# Optimizing a Trainium2 kernel written in Bass

```python
import numpy as np
import jax
import jax.numpy as jnp

def _softmax(x, axis=-1):
    return jax.nn.softmax(x, axis=axis)

def _gelu(x):
    return jax.nn.gelu(x, approximate=True)

def _silu(x):
    return jax.nn.silu(x)

def _sigmoid(x):
    return jax.nn.sigmoid(x)

def _layernorm(x, axis=-1, eps=1e-05):
    m = jnp.mean(x, axis=axis, keepdims=True)
    v = jnp.var(x, axis=axis, keepdims=True)
    return (x - m) / jnp.sqrt(v + eps)

def _scatter_add(tgt, idx, src, axis=0):
    return tgt.at[idx].add(src)

def _segment_sum(src, seg, n):
    return jax.ops.segment_sum(src, seg, n)
kernel_name = 'mk_gnn_resnorm_d4_gnn_r8_3c7a00'

def setup_inputs(seed: int=0):
    np.random.seed(seed)
    _w = jnp.asarray

    def _rec_inputs():
        import jax
        import jax.numpy as jnp
        _gk = jax.random.key(seed)
        x = -0.000202 + 1 * jax.random.normal(jax.random.fold_in(_gk, 1), (6250, 128), jnp.float32)
        src = jax.random.randint(jax.random.fold_in(_gk, 2), (100000,), 0, 6250, jnp.int32)
        dst = jnp.minimum((6250 * jax.random.uniform(jax.random.fold_in(_gk, 3), (100000,)) ** 2.0).astype(jnp.int32), 49999)
        _o = jnp.argsort(dst, stable=True)
        src = src[_o]
        dst = dst[_o]
        edge_attr_8 = 0.000254156 + 0.999948 * jax.random.normal(jax.random.fold_in(_gk, 12), (100000, 8), jnp.float32)
        edge_weight = jax.random.uniform(jax.random.fold_in(_gk, 14), (100000,), jnp.float32, 0.0, 0.999998)
        return (x, src, dst, edge_attr_8, edge_weight)
    x, src, dst, edge_attr_8, edge_weight = _rec_inputs()

    def _L0_gnn_setup():
        import jax, jax.numpy as jnp
        import numpy as np
        N_NODES = 6250
        N_EDGES = 100000
        D = 128

        def _gcn_norm(edge_index, edge_weights, n_nodes):
            src = jnp.concatenate([edge_index[0], jnp.arange(n_nodes)])
            dst = jnp.concatenate([edge_index[1], jnp.arange(n_nodes)])
            w = jnp.concatenate([edge_weights, jnp.ones((n_nodes,), edge_weights.dtype)])
            deg = jax.ops.segment_sum(w, dst, num_segments=n_nodes)
            dinv = jnp.where(deg > 0, jax.lax.rsqrt(deg), 0.0)
            norm = dinv[src] * w * dinv[dst]
            return (src, dst, norm)

        def _gcn_conv(x, src, dst, norm, W, b, n_nodes):
            h = x @ W
            msg = h[src] * norm[:, None]
            out = jax.ops.segment_sum(msg, dst, num_segments=n_nodes)
            return out + b
        key = jax.random.key(seed)
        ks = jax.random.split(key, 12)
        s = 1.0 / np.sqrt(D)
        return {'x': jax.random.normal(ks[0], (N_NODES, D), jnp.float32), 'edge_index': jax.random.randint(ks[1], (2, N_EDGES), 0, N_NODES, jnp.int64), 'edge_weights': jax.random.uniform(ks[2], (N_EDGES,), jnp.float32), 'W1': jax.random.normal(ks[3], (D, D), jnp.float32) * s, 'b1': jnp.zeros((D,), jnp.float32), 'W2': jax.random.normal(ks[4], (D, D), jnp.float32) * s, 'b2': jnp.zeros((D,), jnp.float32), 'W3': jax.random.normal(ks[5], (D, D), jnp.float32) * s, 'b3': jnp.zeros((D,), jnp.float32), 'Wl': jax.random.normal(ks[6], (D, D), jnp.float32) * s, 'bl': jnp.zeros((D,), jnp.float32)}
    _L0_gnn_all = _L0_gnn_setup()
    _L0_gnn_in = {k: v for k, v in _L0_gnn_all.items() if k in ('W1', 'b1', 'W2', 'b2', 'W3', 'b3', 'Wl', 'bl')}
    del _L0_gnn_all

    def _L1_gnn_setup():
        import jax, jax.numpy as jnp
        import numpy as np
        N_NODES = 12500

        def _mean_agg(x, src, dst, n_nodes):
            summed = jax.ops.segment_sum(x[src], dst, num_segments=n_nodes)
            deg = jax.ops.segment_sum(jnp.ones_like(src, dtype=x.dtype), dst, num_segments=n_nodes)
            return summed / jnp.maximum(deg, 1.0)[:, None]

        def _sage_conv(x, src, dst, W_self, W_neigh, b):
            h_neigh = _mean_agg(x, src, dst, x.shape[0])
            return x @ W_self + h_neigh @ W_neigh + b
        key = jax.random.key(seed)
        ks = jax.random.split(key, 8)
        F_IN, F_H, E = (128, 128, 200000)
        s = 1.0 / np.sqrt(F_IN)
        return {'x': jax.random.normal(ks[0], (N_NODES, F_IN), dtype=jnp.float32), 'src': jax.random.randint(ks[1], (E,), 0, N_NODES, dtype=jnp.int64), 'dst': jax.random.randint(ks[2], (E,), 0, N_NODES, dtype=jnp.int64), 'W1_self': jax.random.normal(ks[3], (F_IN, F_H), dtype=jnp.float32) * s, 'W1_neigh': jax.random.normal(ks[4], (F_IN, F_H), dtype=jnp.float32) * s, 'b1': jnp.zeros((F_H,), dtype=jnp.float32), 'W2_self': jax.random.normal(ks[5], (F_H, F_H), dtype=jnp.float32) * s, 'W2_neigh': jax.random.normal(ks[6], (F_H, F_H), dtype=jnp.float32) * s, 'b2': jnp.zeros((F_H,), dtype=jnp.float32)}
    _L1_gnn_all = _L1_gnn_setup()
    _L1_gnn_in = {k: v for k, v in _L1_gnn_all.items() if k in ('W1_self', 'W1_neigh', 'b1', 'W2_self', 'W2_neigh', 'b2')}
    del _L1_gnn_all

    def _L2_gnn_setup():
        import jax, jax.numpy as jnp
        import numpy as np
        N, E, F, H, L = (6250, 75000, 128, 128, 5)
        key = jax.random.key(seed)
        ks = jax.random.split(key, 16)
        s = 1.0 / np.sqrt(H)
        u = lambda k, shape: jax.random.uniform(k, shape, jnp.float32, -s, s)
        return {'x': jax.random.normal(ks[0], (N, F), jnp.float32), 'edge_index': jax.random.randint(ks[1], (2, E), 0, N, jnp.int64), 'enc_w1': u(ks[2], (H, F)), 'enc_b1': u(ks[3], (H,)), 'enc_w2': u(ks[4], (H, H)), 'enc_b2': u(ks[5], (H,)), 'conv_w': u(ks[6], (L, H, H)), 'gru_wih': u(ks[7], (3 * H, H)), 'gru_whh': u(ks[8], (3 * H, H)), 'gru_bih': u(ks[9], (3 * H,)), 'gru_bhh': u(ks[10], (3 * H,)), 'dec_w1': u(ks[11], (H, H)), 'dec_b1': u(ks[12], (H,)), 'dec_w2': u(ks[13], (F, H)), 'dec_b2': u(ks[14], (F,))}
    _L2_gnn_all = _L2_gnn_setup()
    _L2_gnn_in = {k: v for k, v in _L2_gnn_all.items() if k in ('enc_w1', 'enc_b1', 'enc_w2', 'enc_b2', 'conv_w', 'gru_wih', 'gru_whh', 'gru_bih', 'gru_bhh', 'dec_w1', 'dec_b1', 'dec_w2', 'dec_b2')}
    del _L2_gnn_all

    def _L3_gnn_setup():
        import jax, jax.numpy as jnp
        import numpy as np
        N_NODES = 12500
        N_EDGES = 200000
        IN_DIM = 128
        OUT_DIM = 128
        EDGE_IN_DIM = 8
        key = jax.random.key(seed)
        k1, k2, k3, k4 = jax.random.split(key, 4)
        x = jax.random.normal(k1, (N_NODES, IN_DIM), dtype=jnp.float32)
        edge_index = jax.random.randint(k2, (2, N_EDGES), 0, N_NODES, dtype=jnp.int64)
        edge_attr = jax.random.normal(k3, (N_EDGES, EDGE_IN_DIM), dtype=jnp.float32)
        W = jax.random.normal(k4, (IN_DIM, OUT_DIM), dtype=jnp.float32) * (1.0 / np.sqrt(IN_DIM))
        b = jnp.zeros((OUT_DIM,), dtype=jnp.float32)
        return {'x': x, 'edge_index': edge_index, 'edge_attr': edge_attr, 'W': W, 'b': b}
    _L3_gnn_all = _L3_gnn_setup()
    _L3_gnn_in = {k: v for k, v in _L3_gnn_all.items() if k in ('W', 'b')}
    del _L3_gnn_all
    return {'x': x, 'src': src, 'dst': dst, 'edge_attr_8': edge_attr_8, 'edge_weight': edge_weight, 'L0_gnn_W1': _L0_gnn_in['W1'], 'L0_gnn_b1': _L0_gnn_in['b1'], 'L0_gnn_W2': _L0_gnn_in['W2'], 'L0_gnn_b2': _L0_gnn_in['b2'], 'L0_gnn_W3': _L0_gnn_in['W3'], 'L0_gnn_b3': _L0_gnn_in['b3'], 'L0_gnn_Wl': _L0_gnn_in['Wl'], 'L0_gnn_bl': _L0_gnn_in['bl'], 'L1_gnn_W1_self': _L1_gnn_in['W1_self'], 'L1_gnn_W1_neigh': _L1_gnn_in['W1_neigh'], 'L1_gnn_b1': _L1_gnn_in['b1'], 'L1_gnn_W2_self': _L1_gnn_in['W2_self'], 'L1_gnn_W2_neigh': _L1_gnn_in['W2_neigh'], 'L1_gnn_b2': _L1_gnn_in['b2'], 'L2_gnn_enc_w1': _L2_gnn_in['enc_w1'], 'L2_gnn_enc_b1': _L2_gnn_in['enc_b1'], 'L2_gnn_enc_w2': _L2_gnn_in['enc_w2'], 'L2_gnn_enc_b2': _L2_gnn_in['enc_b2'], 'L2_gnn_conv_w': _L2_gnn_in['conv_w'], 'L2_gnn_gru_wih': _L2_gnn_in['gru_wih'], 'L2_gnn_gru_whh': _L2_gnn_in['gru_whh'], 'L2_gnn_gru_bih': _L2_gnn_in['gru_bih'], 'L2_gnn_gru_bhh': _L2_gnn_in['gru_bhh'], 'L2_gnn_dec_w1': _L2_gnn_in['dec_w1'], 'L2_gnn_dec_b1': _L2_gnn_in['dec_b1'], 'L2_gnn_dec_w2': _L2_gnn_in['dec_w2'], 'L2_gnn_dec_b2': _L2_gnn_in['dec_b2'], 'L3_gnn_W': _L3_gnn_in['W'], 'L3_gnn_b': _L3_gnn_in['b']}

def reference(x, src, dst, edge_attr_8, edge_weight, L0_gnn_W1, L0_gnn_b1, L0_gnn_W2, L0_gnn_b2, L0_gnn_W3, L0_gnn_b3, L0_gnn_Wl, L0_gnn_bl, L1_gnn_W1_self, L1_gnn_W1_neigh, L1_gnn_b1, L1_gnn_W2_self, L1_gnn_W2_neigh, L1_gnn_b2, L2_gnn_enc_w1, L2_gnn_enc_b1, L2_gnn_enc_w2, L2_gnn_enc_b2, L2_gnn_conv_w, L2_gnn_gru_wih, L2_gnn_gru_whh, L2_gnn_gru_bih, L2_gnn_gru_bhh, L2_gnn_dec_w1, L2_gnn_dec_b1, L2_gnn_dec_w2, L2_gnn_dec_b2, L3_gnn_W, L3_gnn_b):
    import jax
    import jax.numpy as jnp

    def _L0_gnn_ref(x, edge_index, edge_weights, W1, b1, W2, b2, W3, b3, Wl, bl):
        import jax, jax.numpy as jnp
        import numpy as np
        N_NODES = 6250
        N_EDGES = 100000
        D = 128

        def _gcn_norm(edge_index, edge_weights, n_nodes):
            src = jnp.concatenate([edge_index[0], jnp.arange(n_nodes)])
            dst = jnp.concatenate([edge_index[1], jnp.arange(n_nodes)])
            w = jnp.concatenate([edge_weights, jnp.ones((n_nodes,), edge_weights.dtype)])
            deg = jax.ops.segment_sum(w, dst, num_segments=n_nodes)
            dinv = jnp.where(deg > 0, jax.lax.rsqrt(deg), 0.0)
            norm = dinv[src] * w * dinv[dst]
            return (src, dst, norm)

        def _gcn_conv(x, src, dst, norm, W, b, n_nodes):
            h = x @ W
            msg = h[src] * norm[:, None]
            out = jax.ops.segment_sum(msg, dst, num_segments=n_nodes)
            return out + b
        n = x.shape[0]
        src, dst, norm = _gcn_norm(edge_index, edge_weights, n)
        h = _gcn_conv(x, src, dst, norm, W1, b1, n)
        h = jax.nn.relu(h)
        h = _gcn_conv(h, src, dst, norm, W2, b2, n)
        h = jax.nn.relu(h)
        h = _gcn_conv(h, src, dst, norm, W3, b3, n)
        return h @ Wl + bl

    def _L1_gnn_ref(x, src, dst, W1_self, W1_neigh, b1, W2_self, W2_neigh, b2):
        import jax, jax.numpy as jnp
        import numpy as np
        N_NODES = 12500

        def _mean_agg(x, src, dst, n_nodes):
            summed = jax.ops.segment_sum(x[src], dst, num_segments=n_nodes)
            deg = jax.ops.segment_sum(jnp.ones_like(src, dtype=x.dtype), dst, num_segments=n_nodes)
            return summed / jnp.maximum(deg, 1.0)[:, None]

        def _sage_conv(x, src, dst, W_self, W_neigh, b):
            h_neigh = _mean_agg(x, src, dst, x.shape[0])
            return x @ W_self + h_neigh @ W_neigh + b
        h = _sage_conv(x, src, dst, W1_self, W1_neigh, b1)
        h = jax.nn.relu(h)
        return _sage_conv(h, src, dst, W2_self, W2_neigh, b2)

    def _L2_gnn_ref(x, edge_index, enc_w1, enc_b1, enc_w2, enc_b2, conv_w, gru_wih, gru_whh, gru_bih, gru_bhh, dec_w1, dec_b1, dec_w2, dec_b2):
        import jax, jax.numpy as jnp
        import numpy as np
        N, E, F, H, L = (6250, 75000, 128, 128, 5)
        src, dst = (edge_index[0], edge_index[1])
        n_nodes = x.shape[0]
        h = jnp.maximum(x @ enc_w1.T + enc_b1, 0.0) @ enc_w2.T + enc_b2

        def step(h, w):
            m = h @ w
            agg = jax.ops.segment_sum(m[src], dst, num_segments=n_nodes)
            gi = agg @ gru_wih.T + gru_bih
            gh = h @ gru_whh.T + gru_bhh
            ir, iz, i_n = jnp.split(gi, 3, axis=1)
            hr, hz, h_n = jnp.split(gh, 3, axis=1)
            r = jax.nn.sigmoid(ir + hr)
            z = jax.nn.sigmoid(iz + hz)
            n = jnp.tanh(i_n + r * h_n)
            return ((1.0 - z) * n + z * h, None)
        h, _ = jax.lax.scan(step, h, conv_w)
        h = jnp.maximum(h, 0.0)
        out = jnp.maximum(h @ dec_w1.T + dec_b1, 0.0) @ dec_w2.T + dec_b2
        return jax.nn.sigmoid(out)

    def _L3_gnn_ref(x, edge_index, edge_attr, W, b):
        import jax, jax.numpy as jnp
        import numpy as np
        N_NODES = 12500
        N_EDGES = 200000
        IN_DIM = 128
        OUT_DIM = 128
        EDGE_IN_DIM = 8
        N = x.shape[0]
        loop = jnp.arange(N, dtype=edge_index.dtype)
        src = jnp.concatenate([edge_index[0], loop])
        dst = jnp.concatenate([edge_index[1], loop])
        deg = jax.ops.segment_sum(jnp.ones_like(dst, dtype=x.dtype), dst, num_segments=N)
        dinv = jnp.where(deg > 0, jax.lax.rsqrt(deg), 0.0)
        norm = dinv[src] * dinv[dst]
        xw = x @ W
        msgs = xw[src] * norm[:, None]
        out = jax.ops.segment_sum(msgs, dst, num_segments=N)
        return out + b
    edge_index = jnp.stack([src, dst])
    x = _layernorm(x + _L0_gnn_ref(x, edge_index, edge_weight, L0_gnn_W1, L0_gnn_b1, L0_gnn_W2, L0_gnn_b2, L0_gnn_W3, L0_gnn_b3, L0_gnn_Wl, L0_gnn_bl), axis=-1)
    x = _layernorm(x + _L1_gnn_ref(x, src, dst, L1_gnn_W1_self, L1_gnn_W1_neigh, L1_gnn_b1, L1_gnn_W2_self, L1_gnn_W2_neigh, L1_gnn_b2), axis=-1)
    x = _layernorm(x + _L2_gnn_ref(x, edge_index, L2_gnn_enc_w1, L2_gnn_enc_b1, L2_gnn_enc_w2, L2_gnn_enc_b2, L2_gnn_conv_w, L2_gnn_gru_wih, L2_gnn_gru_whh, L2_gnn_gru_bih, L2_gnn_gru_bhh, L2_gnn_dec_w1, L2_gnn_dec_b1, L2_gnn_dec_w2, L2_gnn_dec_b2), axis=-1)
    x = _layernorm(x + _L3_gnn_ref(x, edge_index, edge_attr_8, L3_gnn_W, L3_gnn_b), axis=-1)
    return x

_drawn_inputs = setup_inputs


def setup_inputs(seed=0):
    import zlib

    import numpy as np

    out = dict(_drawn_inputs(seed))
    spreads = {'L0_gnn_b1': (0.0, 0.1),
     'L0_gnn_b2': (0.0, 0.1),
     'L0_gnn_b3': (0.0, 0.1),
     'L0_gnn_bl': (0.0, 0.1),
     'L1_gnn_b1': (0.0, 0.1),
     'L1_gnn_b2': (0.0, 0.1),
     'L3_gnn_b': (0.0, 0.1)}
    factors = {'edge_weight': 26.696,
     'L2_gnn_enc_w1': 3.34,
     'L2_gnn_enc_b1': 7.402,
     'L2_gnn_enc_w2': 2.741,
     'L2_gnn_enc_b2': 2.845,
     'L2_gnn_conv_w': 2.881,
     'L2_gnn_gru_whh': 5.601,
     'L2_gnn_gru_bih': 7.05,
     'L2_gnn_gru_bhh': 8.0,
     'L2_gnn_dec_w1': 2.679,
     'L2_gnn_dec_b1': 8.0,
     'L2_gnn_dec_b2': 3.777}
    for name, (base, spread) in spreads.items():
        noise = np.random.default_rng([zlib.crc32(name.encode()), seed]).standard_normal(out[name].shape)
        drawn = base * np.exp(spread * noise) if base else spread * noise
        out[name] = jnp.asarray(drawn.astype(out[name].dtype))
    for name, factor in factors.items():
        out[name] = (out[name] * factor).astype(out[name].dtype)
    return out
```

```python
from contextlib import ExitStack, contextmanager

import concourse.bass as bass
from concourse import mybir

F32, BF16, F16 = mybir.dt.float32, mybir.dt.bfloat16, mybir.dt.float16
I32, U16 = mybir.dt.int32, mybir.dt.uint16
ALU, ACT, AX = mybir.AluOpType, mybir.ActivationFunctionType, mybir.AxisListType.X
ds = bass.ds

P = 128
D = 128
N = 6250
E = 100000
CHUNKS = -(-N // P)
NP = CHUNKS * P
TAIL = N - (CHUNKS - 1) * P
STEPS = 5
EPS = 1e-5

EP = 125
TILES = E // EP
TB = 8
B = EP * TB
NB = E // B
DUMP = NP * NP
SPARE = 1024
KEY_BIT = 0x20000000

BANK = 512
BLOCKS = -(-NP // BANK)
RING = 7
LAPS = CHUNKS // RING
SWEEPS32 = ((0, 5), (5, 4), (9, 4))
SWEEPS16 = ((0, 7), (7, 6))
SLOT32 = 5 * BANK
SLOT16 = 7 * BANK
G = 7
GROUPS = CHUNKS // G

LN_SCALE = 1024.0
WEIGHTS = ("W1", "W2", "W3T", "Wl", "W1s", "W1n", "W2s", "W2n", "E1T", "E2T", "D1T", "D2T", "L3W",
           "wihT0", "wihT1", "wihT2", "whhT0", "whhT1", "whhT2", "cT0", "cT1", "cT2", "cT3", "cT4")
ROWS = ("b1", "b2", "bl", "sb1", "sb2", "db2", "b4")
COLS = ("b3", "eb1", "eb2", "bi0", "bi1", "bi2", "bh0", "bh1", "bh2", "db1")


def block_width(b):
    return min(BANK, NP - b * BANK)


class Count:

    def __init__(self, eng, sem):
        self.eng, self.sem, self.n, self.over = eng, sem, 0, None

    def mark(self, ins):
        ins.then_inc(self.sem, 1)
        self.n += 1

    def value(self, back=0):
        n = self.n - back
        return n if self.over is None else self.over[0] * self.over[1] + n

    def wait(self, back=0):
        self.eng.wait_ge(self.sem, self.value(back))

    @contextmanager
    def loop(self, start, end, per):
        base = self.n
        with self.eng.Fori(start, end) as i:
            self.over, self.n = (i, per), base - start * per
            yield i
            assert self.n == base - start * per + per, (self.n, base, per)
        self.over, self.n = None, base + (end - start) * per


def carve(arena):
    at = [0]

    def take(parts, shape, dtype):
        size = 1
        for s in shape:
            size *= s
        words = -(-size * (2 if dtype in (BF16, F16, U16) else 4) // 32) * 8
        ap = arena[0:parts, at[0]:at[0] + words]
        at[0] += words
        assert at[0] <= arena.shape[1], at[0]
        if dtype != F32:
            ap = ap.bitcast(dtype)
        ap = ap[:, 0:size]
        if len(shape) > 1:
            names = "abcd"[:len(shape)]
            ap = ap.rearrange(f"p ({' '.join(names)}) -> p {' '.join(names)}",
                              **{n: s for n, s in zip(names, shape)})
        return ap
    return take, at


def build_adjacency(nc, io, sems, persist, take, psum):
    src, dst, ew, W_adj, C_adj, keys = (io[k] for k in ("src", "dst", "ew", "W_adj", "C_adj", "keys"))
    idx, cnt, deg = persist["idx"], persist["cnt"], persist["deg"]
    psS = psum[:, 0:3, :]
    psD = psum[:, 3, :]
    zero = take(P, [NP], F32)
    ends = take(EP, [2, TILES], I32)
    w = take(EP, [TILES], F32)
    cell, key, tmp, tmp2, flip, spare = (take(EP, [TILES], I32) for _ in range(6))
    spare0 = take(EP, [TB], I32)
    dlo, dhi = take(EP, [TILES], BF16), take(EP, [TILES], BF16)
    V = take(EP, [TILES, 5], BF16)
    rest = take(EP, [TILES], F32)
    ramp, rampb = take(P, [P], F32), take(P, [P], BF16)
    pcol = take(P, [1], F32)
    earlier = take(EP, [EP], BF16)
    krow = take(EP, [3, B], F32)
    Eq = take(EP, [3, TB * (B + 1)], BF16)
    Et = take(EP, [3, TB, EP], BF16)
    ohl, ohh, ohv = take(EP, [3, TB, P], BF16), take(EP, [3, TB, CHUNKS], BF16), take(EP, [3, TB, 4, CHUNKS], BF16)
    mask = take(EP, [TB], I32)
    wsum = take(EP, [TILES], F32)
    cell_slot, w_slot = take(EP, [2, TB], I32), take(EP, [2, TB], F32)
    nudge = take(EP, [8], F32)
    names = "edges_in ramps zero_set c_zeroed key_set keys_out row_used equal_set batch_counted cell_set " \
            "w_added slot_filled dve_step merged hot_set"
    s = {n: sems(n) for n in names.split()}
    row_in = [sems(f"row_in{i}") for i in range(3)]
    w_zeroed = [sems(f"w_zeroed{i}") for i in range(2)]

    block = nc.Block()
    with block:
        @block.sync
        def _(sp):
            for to, of in ((ends[:, 0, :], src), (ends[:, 1, :], dst), (w, ew)):
                sp.dma_start(to, of.rearrange("(p t) -> p t", t=TILES)).then_inc(s["edges_in"], 16)
            sp.wait_ge(s["keys_out"], 16)
            sp.wait_ge(s["zero_set"], 1)
            W_rows = W_adj[0:DUMP, :].rearrange("(r c) o -> r (c o)", c=NP)
            for u in range(2):
                sp.dma_start(W_rows[u * P:(u + 1) * P, :], zero).then_inc(w_zeroed[u], 16)
            with sp.Fori(1, CHUNKS // 2) as k:
                for u in range(2):
                    sp.wait_ge(w_zeroed[u], 16 * k)
                    sp.dma_start(W_rows[ds((2 * k + u) * P, P), :], zero).then_inc(w_zeroed[u], 16)
            sp.dma_start(W_rows[NP - P:, :], zero).then_inc(w_zeroed[0], 16)
            sp.dma_start(W_adj[DUMP:DUMP + SPARE, :].rearrange("(p c) o -> p (c o)", c=8),
                         zero[:, 0:8]).then_inc(w_zeroed[1], 16)
            for u in range(2):
                sp.wait_ge(w_zeroed[u], 16 * (CHUNKS // 2 + 1))
            C_rows = C_adj[0:DUMP, :].rearrange("(r c) o -> r (c o)", c=NP)
            z16 = zero[0:P // 2, 0:NP // 2].bitcast(F16)
            sp.dma_start(C_adj[DUMP:DUMP + SPARE, :].rearrange("(p c) o -> p (c o)", c=16),
                         z16[:, 0:16]).then_inc(s["c_zeroed"], 16)
            with sp.Fori(0, 2 * CHUNKS) as k:
                sp.wait_ge(s["c_zeroed"], 16 * k + 16)
                sp.dma_start(C_rows[ds(k * (P // 2), P // 2), :], z16).then_inc(s["c_zeroed"], 16)
            sp.wait_ge(s["c_zeroed"], 16 * (2 * CHUNKS + 1))

        @block.scalar
        def _(act):
            act.wait_ge(s["key_set"], 1)
            act.dma_start(keys.rearrange("b p j -> p b j"),
                          key.rearrange("p (b j) -> p b j", j=TB)).then_inc(s["keys_out"], 16)
            act.wait_ge(s["keys_out"], 16)
            rows = keys.rearrange("b p j -> b (p j)")

            def row(b, slot):
                act.dma_start(krow[:, slot, :].bitcast(I32),
                              rows[ds(b, 1), :].to_broadcast([EP, B])).then_inc(row_in[slot], 16)

            for b in range(3):
                row(b, b)
            with act.Fori(0, (NB - 4) // 3) as i:
                for u in range(3):
                    act.wait_ge(s["row_used"], 3 * i + u + 1)
                    row(3 * i + 3 + u, u)
            act.wait_ge(s["row_used"], NB - 3)
            row(NB - 1, (NB - 1) % 3)

        @block.gpsimd
        def _(pool):
            for to, step in ((ramp, 0), (pcol, 1)):
                pool.iota(to, [[1, to.shape[1]]], base=0, channel_multiplier=step,
                          allow_small_or_imprecise_dtypes=True).then_inc(s["ramps"], 1)
            pool.iota(spare0, [[1, TB]], base=0, channel_multiplier=TB).then_inc(s["ramps"], 1)
            pool.memset(nudge, 0.0).then_inc(s["ramps"], 1)
            pool.wait_ge(s["ramps"], 4)
            for u in range(2):
                pool.wait_ge(w_zeroed[u], 16 * (CHUNKS // 2 + 1))
            add_batches(pool, W_adj, idx, wsum, F32, cell_slot, w_slot, nudge,
                        s["cell_set"], s["slot_filled"], s["w_added"])

        @block.vector
        def _(dve):
            step = Count(dve, s["dve_step"])

            def link(ins):
                step.mark(ins)
                step.wait()

            dve.memset(zero, 0.0).then_inc(s["zero_set"], 1)
            dve.wait_ge(s["edges_in"], 48)
            link(dve.tensor_scalar(tmp, ends[:, 0, :], float(CHUNKS), None, ALU.mult))
            link(dve.tensor_scalar(tmp2, ends[:, 1, :], 7, None, ALU.logical_shift_right))
            dve.tensor_copy(dhi, tmp2)
            link(dve.tensor_tensor(tmp, tmp, tmp2, ALU.add))
            link(dve.tensor_scalar(tmp, tmp, 7, None, ALU.logical_shift_left))
            link(dve.tensor_scalar(tmp2, ends[:, 1, :], P - 1, None, ALU.bitwise_and))
            dve.tensor_copy(dlo, tmp2)
            link(dve.tensor_tensor(cell, tmp, tmp2, ALU.bitwise_or))
            dve.tensor_scalar(key, cell, KEY_BIT, None, ALU.bitwise_or).then_inc(s["key_set"], 1)
            dve.wait_ge(s["ramps"], 4)
            link(dve.tensor_scalar(spare0, spare0, DUMP, None, ALU.bitwise_or))
            link(dve.tensor_copy(spare.bitcast(U16).rearrange("p (b j) -> p b j", j=2 * TB),
                                 spare0.bitcast(U16).unsqueeze(1).to_broadcast([EP, NB, 2 * TB])))
            dve.tensor_tensor(flip, cell, spare, ALU.bitwise_xor)
            link(dve.tensor_copy(V[:, :, 0], w))
            link(dve.tensor_tensor(rest, w, V[:, :, 0], ALU.subtract))
            link(dve.tensor_copy(V[:, :, 1], rest))
            link(dve.tensor_tensor(rest, rest, V[:, :, 1], ALU.subtract))
            dve.tensor_copy(V[:, :, 2], rest)
            dve.memset(V[:, :, 3:5], 1.0)
            dve.tensor_copy(rampb, ramp)
            dve.memset(Eq.rearrange("p a b -> p (a b)"), 0.0)
            link(dve.tensor_scalar(earlier, ramp[0:EP, 0:EP], pcol[0:EP, 0:1], None, ALU.is_gt))
            keyf = key.bitcast(F32)

            def compare(b, slot, arrivals):
                dve.wait_ge(row_in[slot], 16 * arrivals)
                if not isinstance(b, int) or b >= 3:
                    dve.wait_ge(s["batch_counted"], b - 2)
                for j in range(TB):
                    ins = dve.tensor_scalar(Eq[:, slot, j * B:(j + 1) * B], krow[:, slot, :],
                                            keyf[:, ds(b * TB + j, 1)], None, ALU.is_equal)
                ins.then_inc(s["row_used"], 1)
                dve.tensor_tensor(ohl[:, slot], rampb[0:EP, :].unsqueeze(1).to_broadcast([EP, TB, P]),
                                  dlo[:, ds(b * TB, TB)].unsqueeze(2).to_broadcast([EP, TB, P]), ALU.is_equal)
                dve.tensor_tensor(ohh[:, slot], rampb[0:EP, 0:CHUNKS].unsqueeze(1).to_broadcast([EP, TB, CHUNKS]),
                                  dhi[:, ds(b * TB, TB)].unsqueeze(2).to_broadcast([EP, TB, CHUNKS]),
                                  ALU.is_equal).then_inc(s["hot_set"], 1)
                dve.wait_ge(s["row_used"], b + 1)
                own = Eq[:, slot, :].rearrange("p (j k) -> p j k", k=B + 1)[:, :, 0:B] \
                    .rearrange("p j (q i) -> p j q i", i=TB)[:, :, :, 0]
                dve.tensor_tensor(Et[:, slot], own, earlier.unsqueeze(1).to_broadcast([EP, TB, EP]), ALU.mult)
                dve.wait_ge(s["hot_set"], b + 1)
                dve.tensor_tensor(ohv[:, slot], ohh[:, slot].unsqueeze(2).to_broadcast([EP, TB, 4, CHUNKS]),
                                  V[:, ds(b * TB, TB), 0:4].unsqueeze(3).to_broadcast([EP, TB, 4, CHUNKS]),
                                  ALU.mult).then_inc(s["equal_set"], 1)

            def merge(b, slot):
                dve.wait_ge(s["batch_counted"], b + 1)
                sums = psS[0:EP, slot, 0:TB * 5].rearrange("p (i c) -> p i c", c=5)
                at = ds(b * TB, TB)
                dve.tensor_reduce(wsum[:, at], sums[:, :, 0:3], AX, ALU.add)
                dve.tensor_copy(cnt[:, at], sums[:, :, 3])
                if not isinstance(b, int) or b >= 1:
                    dve.wait_ge(s["cell_set"], b)
                dve.tensor_scalar(mask, sums[:, :, 4], 0.0, -1.0, ALU.is_equal, ALU.mult).then_inc(s["merged"], 1)
                dve.wait_ge(s["merged"], 2 * b + 1)
                dve.tensor_tensor(mask, mask, flip[:, at], ALU.bitwise_and).then_inc(s["merged"], 1)
                dve.wait_ge(s["merged"], 2 * b + 2)
                dve.tensor_tensor(idx[:, at], mask, spare[:, at], ALU.bitwise_xor).then_inc(s["cell_set"], 1)

            compare(0, 0, 1)
            for b in range(3):
                compare(b + 1, (b + 1) % 3, 1 + (b == 2))
                merge(b, b)
            with dve.Fori(1, NB // 3) as i:
                for u in range(3):
                    compare(3 * i + 1 + u, (1 + u) % 3, i + 1 + (u == 2))
                    merge(3 * i + u, u)
            merge(NB - 1, (NB - 1) % 3)
            parts = psD[:, 0:4 * CHUNKS].rearrange("p (c k) -> p c k", c=4)
            link(dve.tensor_copy(deg[:, 0:4, :], parts))
            link(dve.tensor_tensor(deg[:, 0, :], deg[:, 0, :], deg[:, 1, :], ALU.add))
            link(dve.tensor_tensor(deg[:, 0, :], deg[:, 0, :], deg[:, 2, :], ALU.add))

        @block.tensor
        def _(pe):
            pe.wait_ge(s["zero_set"], 1)
            pe.matmul(psD[:, 0:4 * CHUNKS], zero[:, 0:P], zero[:, 0:4 * CHUNKS], start=True, stop=False,
                      skip_group_check=True)

            def batch(b, slot):
                pe.wait_ge(s["equal_set"], b + 1)
                if not isinstance(b, int) or b >= 3:
                    pe.wait_ge(s["cell_set"], b - 2)
                for i in range(TB):
                    for j in range(TB):
                        same = Eq[:, slot, j * B:(j + 1) * B].rearrange("p (q i) -> p q i", i=TB)[:, :, i]
                        n = 5 if j < i else 4
                        pe.matmul(psS[0:EP, slot, 5 * i:5 * i + n], same,
                                  V[:, ds(b * TB + j, 1), 0:n].rearrange("p a c -> p (a c)"),
                                  start=(j == 0), stop=False, skip_group_check=True)
                    pe.matmul(psS[0:EP, slot, 5 * i + 4:5 * i + 5], Et[:, slot, i, :], V[:, 0, 4:5],
                              start=False, stop=(i == TB - 1), skip_group_check=True)
                for j in range(TB):
                    ins = pe.matmul(psD[:, 0:4 * CHUNKS], ohl[:, slot, j, :],
                                    ohv[:, slot, j].rearrange("p c k -> p (c k)"),
                                    start=False, stop=False, skip_group_check=True)
                ins.then_inc(s["batch_counted"], 1)

            for b in range(4):
                batch(b, b % 3)
            with pe.Fori(1, NB // 3) as i:
                for u in range(3):
                    batch(3 * i + 1 + u, (1 + u) % 3)


def add_batches(pool, table, idx, values, dtype, cell_slot, value_slot, nudge, cell_set, slot_filled, added):
    idx16 = idx.bitcast(U16)
    slots16 = cell_slot.rearrange("p a b -> p (a b)").bitcast(U16)

    def batch(b, slot, first=False):
        if cell_set is not None:
            pool.wait_ge(cell_set, b + 1)
        pool.tensor_copy(slots16[:, slot * 2 * TB:(slot + 1) * 2 * TB],
                         idx16[:, ds(b * 2 * TB, 2 * TB)]).then_inc(slot_filled, 1)
        pool.tensor_copy(value_slot[:, slot, :], values[:, ds(b * TB, TB)]).then_inc(slot_filled, 1)
        pool.wait_ge(slot_filled, 3 * b + 2)
        if not first:
            pool.wait_ge(added, 16 * TB * b)
        pool.tensor_tensor(nudge, nudge, nudge, ALU.add).then_inc(slot_filled, 1)
        pool.wait_ge(slot_filled, 3 * b + 3) if first else None
        for j in range(TB):
            pool.indirect_dma_start(table, bass.IndirectOffsetOnAxis(cell_slot[:, slot, j:j + 1], 0),
                                    value_slot[:, slot, j:j + 1], None, compute_op=ALU.add).then_inc(added, 16)

    batch(0, 0, True)
    batch(1, 1)
    with pool.Fori(1, NB // 2) as i:
        batch(2 * i, 0)
        batch(2 * i + 1, 1)
    pool.wait_ge(added, 16 * TB * NB)


def run_layers(nc, io, sems, persist, take, at, psum):
    W_adj, C_adj = io["W_adj"], io["C_adj"]
    idx, cnt, deg = persist["idx"], persist["cnt"], persist["deg"]
    top = at[0]
    ring32 = take(P, [RING, SLOT32], F32)
    at[0] = top
    ring16 = take(P, [RING, SLOT16], F16)
    h_fm = take(P, [NP], F32)
    x_nm = take(P, [CHUNKS, D], F32)
    top = at[0]
    h_nm = take(P, [CHUNKS, D], F32)
    at[0] = top
    h_parts = take(P, [2, NP], F16)
    at[0] = top
    gate_r, gate_z, pre_n, new_n, diff = (take(P, [2, BANK], F32) for _ in range(5))
    at[0] = top + NP
    sum_fm = take(P, [NP], F32)
    stage = take(P, [RING, D], F32)
    weights = take(P, [len(WEIGHTS), D], F32)
    wt = {n: weights[:, i, :] for i, n in enumerate(WEIGHTS)}
    rows = take(P, [len(ROWS), D], F32)
    row = {n: rows[:, i, :] for i, n in enumerate(ROWS)}
    cols = take(P, [len(COLS)], F32)
    col = {n: cols[:, i:i + 1] for i, n in enumerate(COLS)}
    br, bz = take(P, [1], F32), take(P, [1], F32)
    W3l, b3wide, gates = take(P, [D], F32), take(P, [D], F32), take(P, [3 * D], F32)
    row3l = take(P, [D], F32)
    ident, ident16 = take(P, [P], F32), take(P, [P], F16)
    dinv_w, dinv_c, rdeg, dmask = (take(P, [CHUNKS], F32) for _ in range(4))
    tA, tB = take(P, [G, D], F32), take(P, [G, D], F32)
    stats, meanvar = take(P, [G, 6], F32), take(P, [G, 2], F32)
    std, rstd = take(P, [G], F32), take(P, [G], F32)
    eps = take(P, [1], F32)
    extremes, peak, top_abs = take(P, [2], F32), take(P, [2], F32), take(P, [1], F32)
    expo, expo2 = take(P, [1], I32), take(P, [1], I32)
    up, down = take(P, [2], F32), take(P, [2], F32)
    cell_slot, c_slot = take(EP, [2, TB], I32), take(EP, [2, TB], F16)
    nudge = take(EP, [8], F32)
    tick = take(P, [8], F32)

    names = "loaded ident_set slot_filled c_added chunk_used staged swept sum_dve sum_act full free hi_set " \
            "var_set std_set gates_set new_set dve_step act_step dve_stage act_stage ext_set peak_set out_written " \
            "pad_zeroed b3_spread deg_set deg_root"
    s = {n: sems("l_" + n) for n in names.split()}
    landed = [sems(f"landed{i}") for i in range(RING)]
    flat = psum.rearrange("p b c -> p (b c)")
    group_ps = [flat[:, q * 2 * BANK:q * 2 * BANK + G * D] for q in range(4)]

    stages = [("setup", None)]
    for n in range(3):
        stages += [("agg32", n), ("gcn", n)]
    stages += [("to_fm_split", None), ("agg16", ("const", None, False)), ("sage1", None), ("nm_to_fm", None),
               ("scale", 0), ("split", 0), ("agg16", ("scaled", 0, False)), ("sage2", None), ("to_fm", None),
               ("encode", 1), ("encode", 2), ("scale", 1), ("split", 1)]
    for n in range(STEPS):
        stages += [("agg16", ("scaled", 1, False)), ("gru", n)] + [("split", 1)] * (n < STEPS - 1)
    stages += [("relu", None), ("decode", 1), ("decode", 2), ("split_scaled", None), ("agg16", ("const", None, True)), ("last", None)]

    def blocks_loop(eng, body):
        with eng.Fori(0, BLOCKS // 2) as i:
            for u in range(2):
                body(2 * i + u, u, BANK)
        body(BLOCKS - 1, 0, block_width(BLOCKS - 1))

    def groups_loop(eng, body):
        with eng.Fori(0, GROUPS // 2) as i:
            for u in range(2):
                body(2 * i + u, u)
        body(GROUPS - 1, 0)

    block = nc.Block()
    with block:
        @block.gpsimd
        def _(pool):
            pool.memset(ident, 1.0).then_inc(s["ident_set"], 1)
            pool.memset(nudge, 0.0)
            pool.wait_ge(s["ident_set"], 1)
            pool.affine_select(out=ident, in_=ident, compare_op=ALU.is_equal, fill=0.0, base=0,
                               pattern=[[-1, P]], channel_multiplier=1).then_inc(s["ident_set"], 1)
            add_batches(pool, C_adj, idx, cnt, F16, cell_slot, c_slot, nudge, None, s["slot_filled"], s["c_added"])
            for n in range(2):
                pool.wait_ge(s["ext_set"], n + 1)
                pool.partition_all_reduce(peak, extremes, P, bass.bass_isa.ReduceOp.absmax).then_inc(s["peak_set"], 1)

        @block.sync
        def _(sp):
            x = io["x"]
            sp.dma_start(x_nm[:, 0:CHUNKS - 1, :],
                         x[0:(CHUNKS - 1) * P, :].rearrange("(c p) f -> p c f", p=P)).then_inc(s["loaded"], 16)
            sp.wait_ge(s["pad_zeroed"], 1)
            sp.dma_start(x_nm[0:TAIL, CHUNKS - 1, :], x[(CHUNKS - 1) * P:, :]).then_inc(s["loaded"], 16)
            sp.dma_start(weights, io["weights"].rearrange("w p f -> p w f")).then_inc(s["loaded"], 16)
            sp.dma_start(rows, io["rows"].rearrange("r f -> (r f)").unsqueeze(0).to_broadcast([P, len(ROWS) * D])
                         .rearrange("p (r f) -> p r f", f=D)).then_inc(s["loaded"], 16)
            sp.dma_start(cols, io["cols"]).then_inc(s["loaded"], 16)
            used = lap = 0
            for kind, arg in stages:
                if not kind.startswith("agg"):
                    continue
                wide = kind == "agg32"
                table, ring = (W_adj, ring32) if wide else (C_adj, ring16)
                table = table[0:DUMP, :].rearrange("(r c) o -> r (c o)", c=NP)
                if not wide and arg[0] == "const" and not arg[2]:
                    sp.wait_ge(s["chunk_used"], used)
                    sp.wait_ge(s["c_added"], 16 * TB * NB)
                for first, n in (SWEEPS32 if wide else SWEEPS16):
                    c0 = first * BANK
                    width = min(n * BANK, NP - c0)

                    def load(k, u, held):
                        if held is not None:
                            sp.wait_ge(s["chunk_used"], held)
                        sp.dma_start(ring[:, u, 0:width], table[ds(k * P, P), c0:c0 + width]).then_inc(landed[u], 16)

                    for u in range(RING):
                        load(u, u, used + u + 1 - RING if used else None)
                    with sp.Fori(1, LAPS) as i:
                        for u in range(RING):
                            load(i * RING + u, u, i * RING + (used + u + 1 - RING))
                    used += CHUNKS
            sp.wait_ge(s["act_stage"], len(stages))
            sp.wait_ge(s["dve_stage"], len(stages))
            out = io["out"]
            sp.dma_start(out[0:(CHUNKS - 1) * P, :].rearrange("(c p) f -> p c f", p=P),
                         h_nm[:, 0:CHUNKS - 1, :]).then_inc(s["out_written"], 16)
            sp.dma_start(out[(CHUNKS - 1) * P:, :], h_nm[0:TAIL, CHUNKS - 1, :]).then_inc(s["out_written"], 16)
            sp.wait_ge(s["out_written"], 32)

        @block.tensor
        def _(pe):
            used = Count(pe, s["chunk_used"])
            swept = Count(pe, s["swept"])
            full = Count(pe, s["full"])
            laps = 0
            drained = [0, 0]
            for k, (kind, arg) in enumerate(stages):
                if k:
                    pe.wait_ge(s["dve_stage"], k)
                    pe.wait_ge(s["act_stage"], k)

                def group_products(make):
                    begun = full.n
                    for g in range(GROUPS):
                        if g >= 2:
                            pe.wait_ge(s["free"], begun + g - 1)
                        for c in range(G):
                            ins = make(g * G + c, slice(c * D, (c + 1) * D), g % 2)
                        full.mark(ins)

                def block_products(make):
                    begun = full.n

                    def body(b, u, width):
                        pe.wait_ge(s["free"], b + (begun - 1))
                        make(ds(b * BANK, width), u, width).then_inc(s["full"], 1)

                    for b in range(2):
                        make(ds(b * BANK, BANK), b, BANK).then_inc(s["full"], 1)
                    with pe.Fori(1, BLOCKS // 2) as i:
                        for u in range(2):
                            body(2 * i + u, u, BANK)
                    body(BLOCKS - 1, 0, block_width(BLOCKS - 1))
                    full.n += BLOCKS

                if kind == "setup":
                    pe.wait_ge(s["loaded"], 80)
                    pe.wait_ge(s["b3_spread"], 1)
                    pe.matmul(psum[:, 0, 0:D], wt["W3T"], wt["Wl"], start=True, stop=True)
                    full.mark(pe.matmul(psum[:, 1, 0:D], b3wide, wt["Wl"], start=True, stop=True))
                elif kind in ("agg32", "agg16"):
                    wide = kind == "agg32"
                    selfs = wide or arg[2]
                    ring = ring32 if wide else ring16
                    for sweep, (first, n) in enumerate(SWEEPS32 if wide else SWEEPS16):
                        pe.wait_ge(s["sum_dve"], drained[0]) if drained[0] else None
                        pe.wait_ge(s["sum_act"], drained[1]) if drained[1] else None

                        def chunk(i, u, begin):
                            pe.wait_ge(landed[u], 16 * (laps + 1) if isinstance(i, int) else i * 16 + 16 * (laps + 1))
                            if wide:
                                g = i * RING + (used.n + u + 1)
                                pe.wait_ge(s["staged"], g)
                            for part in range(1 if wide else 2):
                                for b in range(n):
                                    width = block_width(first + b)
                                    lhs = stage[:, u, :] if wide else h_parts[:, part, ds((i * RING + u) * P, P)]
                                    ins = pe.matmul(psum[:, b, 0:width], lhs, ring[:, u, b * BANK:b * BANK + width],
                                                    start=begin and part == 0, stop=False, skip_group_check=True)
                            ins.then_inc(s["chunk_used"], 1)

                        for u in range(RING):
                            chunk(0, u, u == 0)
                        with pe.Fori(1, LAPS) as i:
                            for u in range(RING):
                                chunk(i, u, False)
                        used.n += CHUNKS
                        laps += LAPS
                        if selfs:
                            for c in range(first * 4, min((first + n) * 4, CHUNKS)):
                                to = psum[:, c // 4 - first, c % 4 * P:c % 4 * P + P]
                                if wide:
                                    ins = pe.matmul(to, h_nm[:, c, :], ident, start=False, stop=False,
                                                    skip_group_check=True)
                                else:
                                    for part in range(2):
                                        ins = pe.matmul(to, h_parts[:, part, c * P:(c + 1) * P], ident16,
                                                        start=False, stop=False, skip_group_check=True)
                            swept.mark(ins)
                        if wide:
                            drained[0] += n
                        else:
                            drained[0] += n // 2
                            drained[1] += (n + 1) // 2
                elif kind == "gcn":
                    rhs = (wt["W1"], wt["W2"], W3l)[arg]
                    group_products(lambda c, to, q: pe.matmul(group_ps[q][:, to], sum_fm[:, c * P:(c + 1) * P], rhs,
                                                              start=True, stop=True))
                elif kind in ("sage1", "sage2"):
                    own, neigh = (wt["W1s"], wt["W1n"]) if kind == "sage1" else (wt["W2s"], wt["W2n"])

                    def both(c, to, q):
                        pe.matmul(group_ps[q][:, to], h_fm[:, c * P:(c + 1) * P], own, start=True, stop=True)
                        return pe.matmul(group_ps[2 + q][:, to], sum_fm[:, c * P:(c + 1) * P], neigh,
                                         start=True, stop=True)
                    group_products(both)
                elif kind in ("to_fm_split", "to_fm", "nm_to_fm"):
                    of = h_nm if kind == "nm_to_fm" else x_nm
                    group_products(lambda c, to, q: pe.transpose(group_ps[q][:, to], of[:, c, :], ident))
                elif kind == "split":
                    group_products(lambda c, to, q: pe.transpose(group_ps[q][:, to], h_fm[:, c * P:(c + 1) * P], ident))
                elif kind == "encode" or (kind == "decode" and arg == 1):
                    w_, of = {("encode", 1): ("E1T", h_fm), ("encode", 2): ("E2T", sum_fm),
                              ("decode", 1): ("D1T", h_fm)}[kind, arg]
                    block_products(lambda at_, u, width: pe.matmul(psum[:, 4 * u, 0:width], wt[w_], of[:, at_],
                                                                   start=True, stop=True))
                elif kind == "decode":
                    group_products(lambda c, to, q: pe.matmul(group_ps[q][:, to], sum_fm[:, c * P:(c + 1) * P],
                                                              wt["D2T"], start=True, stop=True))
                elif kind == "gru":
                    full.mark(pe.matmul(psum[:, 7, 0:3 * D], wt[f"cT{arg}"],
                                        weights[:, WEIGHTS.index("wihT0"):WEIGHTS.index("wihT0") + 3, :]
                                        .rearrange("p w f -> p (w f)"), start=True, stop=True))
                    pe.wait_ge(s["free"], full.n)

                    def products(at_, u, width):
                        for gate in range(2):
                            pe.matmul(psum[:, 4 * u + gate, 0:width], gates[:, gate * D:(gate + 1) * D],
                                      sum_fm[:, at_], start=True, stop=False)
                            pe.matmul(psum[:, 4 * u + gate, 0:width], wt[f"whhT{gate}"], h_fm[:, at_],
                                      start=False, stop=True)
                        pe.matmul(psum[:, 4 * u + 2, 0:width], wt["whhT2"], h_fm[:, at_], start=True, stop=True)
                        return pe.matmul(psum[:, 4 * u + 3, 0:width], gates[:, 2 * D:], sum_fm[:, at_],
                                         start=True, stop=True)
                    block_products(products)
                elif kind == "last":
                    group_products(lambda c, to, q: pe.matmul(group_ps[q][:, to], sum_fm[:, c * P:(c + 1) * P],
                                                              wt["L3W"], start=True, stop=True))

        def full_after(kind):
            return {"setup": 1, "gru": 1 + BLOCKS, "encode": BLOCKS}.get(kind, GROUPS)

        def fulls(kind, arg):
            if kind == "setup":
                return 1
            if kind == "gru":
                return 1 + BLOCKS
            if kind == "encode" or (kind, arg) == ("decode", 1):
                return BLOCKS
            if kind in ("agg32", "agg16", "scale", "relu", "split_scaled"):
                return 0
            return GROUPS

        @block.scalar
        def _(act):
            step = Count(act, s["act_step"])
            used = staged = swept = full = drained = hi = stds = news = gated = 0
            for k, (kind, arg) in enumerate(stages):
                if k:
                    act.wait_ge(s["dve_stage"], k)
                    act.wait_ge(s["act_stage"], k)
                if kind == "setup":
                    act.wait_ge(s["loaded"], 80)
                    act.activation(b3wide, col["b3"].to_broadcast([P, D]), ACT.Copy).then_inc(s["b3_spread"], 1)
                    act.wait_ge(s["deg_set"], 2)
                    act.activation(dinv_w, dinv_w, ACT.Sqrt).then_inc(s["deg_root"], 1)
                    act.activation(dinv_c, dinv_c, ACT.Sqrt).then_inc(s["deg_root"], 1)
                elif kind == "agg32":
                    for first, n in SWEEPS32:
                        def copy(i, u):
                            if not (isinstance(i, int) and used == 0):
                                act.wait_ge(s["chunk_used"], i * RING + (used + u + 1 - RING))
                            act.activation(stage[:, u, :], h_nm[:, ds(i * RING + u, 1), :].rearrange("p a f -> p (a f)"),
                                           ACT.Copy).then_inc(s["staged"], 1)
                        for u in range(RING):
                            copy(0, u)
                        with act.Fori(1, LAPS) as i:
                            for u in range(RING):
                                copy(i, u)
                        used += CHUNKS
                    swept += len(SWEEPS32)
                elif kind == "agg16":
                    for first, n in SWEEPS16:
                        used += CHUNKS
                        swept += arg[2]
                        act.wait_ge(s["chunk_used"], used)
                        if arg[2]:
                            act.wait_ge(s["swept"], swept)
                        scale = 1 / LN_SCALE if arg[0] == "const" else down[:, arg[1]:arg[1] + 1]
                        for b in range(0, n, 2):
                            c0, width = (first + b) * BANK, block_width(first + b)
                            act.activation(sum_fm[:, c0:c0 + width], psum[:, b, 0:width], ACT.Copy,
                                           scale=scale).then_inc(s["sum_act"], 1)
                            drained += 1
                elif kind in ("to_fm_split", "to_fm", "nm_to_fm"):
                    def body(g, q):
                        act.wait_ge(s["full"], g + (full + 1))
                        act.activation(h_fm[:, ds(g * (G * D), G * D)], group_ps[q], ACT.Copy).then_inc(s["free"], 1)
                    groups_loop(act, body)
                elif kind == "split":
                    def body(g, q):
                        act.wait_ge(s["full"], g + (full + 1))
                        act.activation(h_parts[:, 0, ds(g * (G * D), G * D)], group_ps[q], ACT.Copy,
                                       scale=up[:, arg:arg + 1]).then_inc(s["hi_set"], 1)
                    groups_loop(act, body)
                elif kind == "encode" or (kind, arg) == ("decode", 1):
                    to, bias, func = {("encode", 1): (sum_fm, "eb1", ACT.Relu), ("encode", 2): (h_fm, "eb2", ACT.Identity),
                                      ("decode", 1): (sum_fm, "db1", ACT.Relu)}[kind, arg]

                    def body(b, u, width):
                        act.wait_ge(s["full"], b + (full + 1))
                        act.activation(to[:, ds(b * BANK, width)], psum[:, 4 * u, 0:width], func,
                                       bias=col[bias]).then_inc(s["free"], 1)
                    blocks_loop(act, body)
                elif kind in ("gcn", "sage2", "last") or (kind, arg) == ("decode", 2):
                    if (kind, arg) in (("gcn", 0), ("gcn", 1)):
                        pass
                    else:
                        def body(g, q):
                            if kind == "decode":
                                act.wait_ge(s["free"], g + (full + 1))
                                act.activation(tB, tA, ACT.Sigmoid).then_inc(s["new_set"], 1)
                            act.wait_ge(s["var_set"], g + (stds + 1))
                            act.activation(std, meanvar[:, :, 1], ACT.Sqrt, bias=eps).then_inc(s["std_set"], 1)
                        groups_loop(act, body)
                        stds += GROUPS
                elif kind == "gru":
                    base = full + 1

                    def body(b, u, width):
                        act.wait_ge(s["full"], b + (base + 1))
                        act.activation(gate_r[:, u, 0:width], psum[:, 4 * u, 0:width], ACT.Sigmoid, bias=br)
                        act.activation(gate_z[:, u, 0:width], psum[:, 4 * u + 1, 0:width], ACT.Sigmoid,
                                       bias=bz).then_inc(s["gates_set"], 1)
                        act.wait_ge(s["free"], b + (base + 1))
                        act.activation(new_n[:, u, 0:width], pre_n[:, u, 0:width], ACT.Tanh,
                                       bias=col["bi2"]).then_inc(s["new_set"], 1)
                    blocks_loop(act, body)
                    gated += BLOCKS
                full += fulls(kind, arg)
                act.activation(tick[:, 0:1], tick[:, 0:1], ACT.Copy).then_inc(s["act_stage"], 1)

        @block.vector
        def _(dve):
            step = Count(dve, s["dve_step"])
            free = Count(dve, s["free"])
            used = full = swept = his = normed = gated = exts = 0

            def link(ins):
                step.mark(ins)
                step.wait()

            def spread(ap):
                return ap.unsqueeze(2).to_broadcast([P, G, D])

            def along(r):
                return r.unsqueeze(1).to_broadcast([P, G, D])

            def invert_sqrt(to, of):
                link(dve.tensor_scalar(dmask, of, 0.0, None, ALU.is_gt))
                link(dve.tensor_scalar(to, of, 1e-34, None, ALU.max))

            for k, (kind, arg) in enumerate(stages):
                if k:
                    dve.wait_ge(s["act_stage"], k)
                    dve.wait_ge(s["dve_stage"], k)
                grouped = fulls(kind, arg)

                def normalise(to, g):
                    for c in range(G):
                        step.mark(dve.bn_stats(stats[:, c, :], tB[:, c, :]))
                    step.wait()
                    dve.tensor_copy(tick[:, 2:3], tick[:, 1:2])
                    for c in range(G - 1):
                        dve.bn_aggr(meanvar[:, c, :], stats[:, c, :])
                    dve.bn_aggr(meanvar[:, G - 1, :], stats[:, G - 1, :]).then_inc(s["var_set"], 1)
                    dve.wait_ge(s["std_set"], g + (normed + 1))
                    link(dve.reciprocal(rstd, std))
                    for c in range(G):
                        ins = dve.tensor_scalar(to[:, ds(g * G + c, 1), :].rearrange("p a f -> p (a f)"), tB[:, c, :],
                                                meanvar[:, c, 0:1], rstd[:, c:c + 1], ALU.subtract, ALU.mult)
                    link(ins)

                if kind == "setup":
                    dve.memset(tick, 0.0)
                    dve.memset(tA.rearrange("p a b -> p (a b)"), 0.0)
                    link(dve.memset(eps, EPS))
                    dve.memset(x_nm[:, CHUNKS - 1, :], 0.0).then_inc(s["pad_zeroed"], 1)
                    link(dve.tensor_scalar(rdeg, deg[:, 3, :], 1.0, None, ALU.max))
                    link(dve.reciprocal(rdeg, rdeg))
                    dve.tensor_scalar(deg[:, 3, :], deg[:, 3, :], 1.0, None, ALU.add)
                    link(dve.tensor_scalar(deg[:, 0, :], deg[:, 0, :], 1.0, None, ALU.add))
                    dve.wait_ge(s["loaded"], 80)
                    dve.tensor_tensor(br, col["bi0"], col["bh0"], ALU.add)
                    dve.tensor_tensor(bz, col["bi1"], col["bh1"], ALU.add)
                    link(dve.tensor_scalar(dmask, deg[:, 0, :], 0.0, None, ALU.is_gt))
                    dve.wait_ge(s["ident_set"], 2)
                    link(dve.tensor_copy(ident16, ident))
                    dve.tensor_scalar(dinv_w, deg[:, 0, :], 1e-34, None, ALU.max).then_inc(s["deg_set"], 1)
                    dve.tensor_scalar(dinv_c, deg[:, 3, :], 1e-34, None, ALU.max).then_inc(s["deg_set"], 1)
                    dve.wait_ge(s["deg_root"], 2)
                    link(dve.reciprocal(dinv_c, dinv_c))
                    link(dve.reciprocal(dinv_w, dinv_w))
                    link(dve.tensor_tensor(dinv_w, dinv_w, dmask, ALU.mult))
                    for g in range(GROUPS):
                        at_ = slice(g * G, (g + 1) * G)
                        link(dve.tensor_tensor(h_nm[:, at_, :], x_nm[:, at_, :], spread(dinv_w[:, at_]), ALU.mult))
                    dve.wait_ge(s["full"], 1)
                    link(dve.tensor_copy(W3l, psum[:, 0, 0:D]))
                    free.mark(dve.tensor_tensor(row3l, psum[:, 1, 0:D], row["bl"], ALU.add))
                elif kind == "agg32":
                    for first, n in SWEEPS32:
                        used += CHUNKS
                        swept += 1
                        dve.wait_ge(s["swept"], swept)
                        for b in range(n):
                            c0, width = (first + b) * BANK, block_width(first + b)
                            dve.tensor_copy(sum_fm[:, c0:c0 + width], psum[:, b, 0:width]).then_inc(s["sum_dve"], 1)
                elif kind == "agg16":
                    for first, n in SWEEPS16:
                        used += CHUNKS
                        swept += arg[2]
                        dve.wait_ge(s["chunk_used"], used)
                        if arg[2]:
                            dve.wait_ge(s["swept"], swept)
                        scale = 1 / LN_SCALE if arg[0] == "const" else down[:, arg[1]:arg[1] + 1]
                        for b in range(1, n, 2):
                            c0, width = (first + b) * BANK, block_width(first + b)
                            dve.tensor_scalar(sum_fm[:, c0:c0 + width], psum[:, b, 0:width], scale, None,
                                              ALU.mult).then_inc(s["sum_dve"], 1)
                elif kind in ("gcn", "sage1", "sage2", "last") or (kind, arg) == ("decode", 2):
                    dinv = dinv_c if kind == "last" else dinv_w
                    bias = {"gcn": (row["b1"], row["b2"], row3l)[arg if kind == "gcn" else 0], "sage1": row["sb1"],
                            "sage2": row["sb2"], "decode": row["db2"], "last": row["b4"]}[kind]
                    norm = kind in ("sage2", "last", "decode") or arg == 2
                    to = h_nm if kind == "last" else x_nm
                    base = free.n

                    def body(g, q):
                        at_ = ds(g * G, G)
                        ps = group_ps[q].rearrange("p (g f) -> p g f", f=D)
                        dve.wait_ge(s["full"], g + (full + 1))
                        if kind in ("gcn", "last"):
                            dve.tensor_tensor(tA, ps, spread(dinv[:, at_]), ALU.mult).then_inc(s["free"], 1)
                            dve.wait_ge(s["free"], g + (base + 1))
                            link(dve.tensor_tensor(tB, tA, along(bias), ALU.add))
                        elif kind in ("sage1", "sage2"):
                            near = group_ps[2 + q].rearrange("p (g f) -> p g f", f=D)
                            link(dve.tensor_tensor(tA, near, spread(rdeg[:, at_]), ALU.mult))
                            dve.tensor_tensor(tB, tA, ps, ALU.add).then_inc(s["free"], 1)
                            dve.wait_ge(s["free"], g + (base + 1))
                            link(dve.tensor_tensor(tB, tB, along(bias), ALU.add))
                        else:
                            dve.tensor_tensor(tA, ps, along(bias), ALU.add).then_inc(s["free"], 1)
                            dve.wait_ge(s["new_set"], g + (gated + 1))
                        if (kind, arg) in (("gcn", 0), ("gcn", 1)):
                            link(dve.scalar_tensor_tensor(out=h_nm[:, at_, :], in0=tB, scalar=0.0,
                                                          in1=spread(dinv[:, at_]), op0=ALU.max, op1=ALU.mult))
                        elif kind == "sage1":
                            link(dve.tensor_scalar(h_nm[:, at_, :], tB, 0.0, None, ALU.max))
                        else:
                            link(dve.tensor_tensor(tB, tB, x_nm[:, at_, :], ALU.add))
                            normalise(to, g)

                    per = 2 if not norm and kind != "sage1" else 3 if not norm else \
                        {"gcn": 2, "last": 2, "sage2": 3, "decode": 1}[kind] + G + 2
                    with step.loop(0, GROUPS // 2, 2 * per) as i:
                        for u in range(2):
                            body(2 * i + u, u)
                    body(GROUPS - 1, 0)
                    free.n += GROUPS
                    if norm:
                        normed += GROUPS
                elif kind in ("to_fm_split", "split_scaled"):
                    for g in range(GROUPS):
                        at_ = slice(g * G, (g + 1) * G)
                        of = x_nm[:, at_, :]
                        if kind == "split_scaled":
                            link(dve.tensor_tensor(tA, of, spread(dinv_c[:, at_]), ALU.mult))
                            of = tA
                        hi, lo = (h_parts[:, p_, :].rearrange("p (c f) -> p c f", f=D)[:, at_, :] for p_ in range(2))
                        link(dve.tensor_scalar(hi, of, LN_SCALE, None, ALU.mult))
                        link(dve.scalar_tensor_tensor(out=lo, in0=of, scalar=LN_SCALE, in1=hi, op0=ALU.mult,
                                                      op1=ALU.subtract))
                    free.n += grouped
                elif kind in ("to_fm", "nm_to_fm", "encode") or (kind, arg) == ("decode", 1):
                    free.n += grouped
                elif kind == "split":
                    def body(g, q):
                        dve.wait_ge(s["hi_set"], g + (his + 1))
                        at_ = ds(g * (G * D), G * D)
                        dve.scalar_tensor_tensor(out=h_parts[:, 1, at_], in0=group_ps[q], scalar=up[:, arg:arg + 1],
                                                 in1=h_parts[:, 0, at_], op0=ALU.mult,
                                                 op1=ALU.subtract).then_inc(s["free"], 1)
                    groups_loop(dve, body)
                    his += GROUPS
                    free.n += GROUPS
                elif kind == "scale":
                    link(dve.tensor_reduce(extremes[:, 0:1], h_fm, AX, ALU.max))
                    dve.tensor_reduce(extremes[:, 1:2], h_fm, AX, ALU.min).then_inc(s["ext_set"], 1)
                    exts += 1
                    dve.wait_ge(s["peak_set"], exts)
                    link(dve.tensor_reduce(top_abs, peak, AX, ALU.max))
                    if arg == 1:
                        link(dve.tensor_scalar(top_abs, top_abs, 1.0, None, ALU.max))
                    link(dve.tensor_scalar(expo, top_abs.bitcast(I32), 23, None, ALU.logical_shift_right))
                    link(dve.tensor_scalar(expo, expo, -1.0, 268.0, ALU.mult, ALU.add))
                    link(dve.tensor_scalar(expo, expo, 240.0, None, ALU.min))
                    link(dve.tensor_scalar(expo2, expo, -1.0, 254.0, ALU.mult, ALU.add))
                    dve.tensor_scalar(up[:, arg:arg + 1].bitcast(I32), expo, 23, None, ALU.logical_shift_left)
                    link(dve.tensor_scalar(down[:, arg:arg + 1].bitcast(I32), expo2, 23, None,
                                           ALU.logical_shift_left))
                elif kind == "gru":
                    dve.wait_ge(s["full"], full + 1)
                    free.mark(dve.tensor_copy(gates, psum[:, 7, 0:3 * D]))
                    base = free.n

                    def body(b, u, width):
                        at_ = ds(b * BANK, width)
                        r, z, pre, new, d_ = (t[:, u, 0:width] for t in (gate_r, gate_z, pre_n, new_n, diff))
                        dve.wait_ge(s["gates_set"], b + (gated + 1))
                        link(dve.scalar_tensor_tensor(out=pre, in0=psum[:, 4 * u + 2, 0:width], scalar=col["bh2"],
                                                      in1=r, op0=ALU.add, op1=ALU.mult))
                        dve.tensor_tensor(pre, pre, psum[:, 4 * u + 3, 0:width], ALU.add).then_inc(s["free"], 1)
                        dve.wait_ge(s["new_set"], b + (gated + 1))
                        link(dve.tensor_tensor(d_, h_fm[:, at_], new, ALU.subtract))
                        link(dve.tensor_tensor(d_, d_, z, ALU.mult))
                        link(dve.tensor_tensor(h_fm[:, at_], d_, new, ALU.add))
                    with step.loop(0, BLOCKS // 2, 8) as i:
                        for u in range(2):
                            body(2 * i + u, u, BANK)
                    body(BLOCKS - 1, 0, block_width(BLOCKS - 1))
                    gated += BLOCKS
                    free.n += BLOCKS
                elif kind == "relu":
                    link(dve.tensor_scalar(h_fm, h_fm, 0.0, None, ALU.max))
                if (kind, arg) == ("decode", 2):
                    gated += GROUPS
                full += grouped
                dve.tensor_copy(tick[:, 1:2], tick[:, 1:2]).then_inc(s["dve_stage"], 1)


def gnn_kernel(nc, io):
    with ExitStack() as ctx:
        arena = ctx.enter_context(nc.sbuf_tensor("arena", [P, 48500], F32))
        psum = ctx.enter_context(nc.psum_tensor("psum", [P, 8, BANK], F32))

        def sems(name):
            return ctx.enter_context(nc.semaphore(name))

        take, at = carve(arena)
        persist = dict(idx=take(EP, [TILES], I32), cnt=take(EP, [TILES], F16), deg=take(P, [4, CHUNKS], F32))
        top = at[0]
        build_adjacency(nc, io, sems, persist, take, psum)
        at[0] = top
        run_layers(nc, io, sems, persist, take, at, psum)


def kernel(**inputs):
    import numpy as np
    import concourse.bacc as bacc
    from concourse.bass_utils import run_bass_kernel_spmd

    a = {k: np.ascontiguousarray(v) for k, v in inputs.items()}
    wih, whh = a["L2_gnn_gru_wih"].reshape(3, D, D), a["L2_gnn_gru_whh"].reshape(3, D, D)
    named = {"W1": a["L0_gnn_W1"], "W2": a["L0_gnn_W2"], "W3T": a["L0_gnn_W3"].T, "Wl": a["L0_gnn_Wl"],
             "W1s": a["L1_gnn_W1_self"], "W1n": a["L1_gnn_W1_neigh"], "W2s": a["L1_gnn_W2_self"],
             "W2n": a["L1_gnn_W2_neigh"], "E1T": a["L2_gnn_enc_w1"].T, "E2T": a["L2_gnn_enc_w2"].T,
             "D1T": a["L2_gnn_dec_w1"].T, "D2T": a["L2_gnn_dec_w2"].T, "L3W": a["L3_gnn_W"]}
    for i in range(3):
        named[f"wihT{i}"], named[f"whhT{i}"] = wih[i].T, whh[i].T
    for i in range(STEPS):
        named[f"cT{i}"] = a["L2_gnn_conv_w"][i].T
    bih, bhh = a["L2_gnn_gru_bih"].reshape(3, D), a["L2_gnn_gru_bhh"].reshape(3, D)
    arrays = {
        "x": a["x"], "src": a["src"], "dst": a["dst"], "ew": a["edge_weight"],
        "weights": np.stack([named[n] for n in WEIGHTS]),
        "rows": np.stack([a["L0_gnn_b1"], a["L0_gnn_b2"], a["L0_gnn_bl"], a["L1_gnn_b1"], a["L1_gnn_b2"],
                          a["L2_gnn_dec_b2"], a["L3_gnn_b"]]),
        "cols": np.ascontiguousarray(np.stack([a["L0_gnn_b3"], a["L2_gnn_enc_b1"], a["L2_gnn_enc_b2"], *bih, *bhh,
                                               a["L2_gnn_dec_b1"]]).T),
    }
    nc = bacc.Bacc("TRN2", target_bir_lowering=False, num_devices=1)
    io = {n: nc.dram_tensor(f"in_{n}", v.shape, mybir.dt.from_np(v.dtype), kind="ExternalInput").ap()
          for n, v in arrays.items()}
    io["out"] = nc.dram_tensor("out", (N, D), F32, kind="ExternalOutput").ap()
    io["W_adj"] = nc.dram_tensor("W_adj", (DUMP + SPARE, 1), F32, kind="Internal").ap()
    io["C_adj"] = nc.dram_tensor("C_adj", (DUMP + SPARE, 1), F16, kind="Internal").ap()
    io["keys"] = nc.dram_tensor("keys", (NB, EP, TB), I32, kind="Internal").ap()
    gnn_kernel(nc, io)
    r = run_bass_kernel_spmd(nc, [{f"in_{n}": v for n, v in arrays.items()}], core_ids=[0])
    return r.results[0]["out"]
```

```python
from contextlib import ExitStack, contextmanager

import concourse.bass as bass
from concourse import mybir

F32, BF16, F16 = mybir.dt.float32, mybir.dt.bfloat16, mybir.dt.float16
I32, U16 = mybir.dt.int32, mybir.dt.uint16
ALU, ACT, AX = mybir.AluOpType, mybir.ActivationFunctionType, mybir.AxisListType.X
ds = bass.ds

P = 128
D = 128
N = 6250
E = 100000
CHUNKS = -(-N // P)
NP = CHUNKS * P
TAIL = N - (CHUNKS - 1) * P
STEPS = 5
EPS = 1e-5
ARENA = 49000

EP = 125
TILES = E // EP
TB = 8
B = EP * TB
NB = E // B
DUMP = NP * NP
SPARE = 1024
KEY_BIT = 0x20000000

BANK = 512
UC = 4
UNITS = -(-CHUNKS // UC)
PAD = UNITS * UC
BLOCKS = UNITS
SWEEPS = ((0, 4, 0), (4, 3, 4), (7, 3, 0), (10, 3, 4))
SLOT = 4 * BANK
LAP = 8
LAPS = (CHUNKS - 1) // LAP
USED0 = LAP

HALF = 0.5
LN_SCALE = 1024.0
WEIGHTS = ("W1", "W2", "W3T", "Wl", "W1s", "W1n", "W2s", "W2n", "E1T", "E2T", "D1T", "D2T", "L3W",
           "wihT0", "wihT1", "wihT2", "whhT0", "whhT1", "whhT2", "cT0", "cT1", "cT2", "cT3", "cT4")
ROWS = ("b1", "b2", "bl", "sb1", "sb2", "db2", "b4")
COLS = ("b3", "eb1", "eb2", "bi0", "bi1", "bi2", "bh0", "bh1", "bh2", "db1")


def block_width(b):
    return min(BANK, NP - b * BANK)


def walk(eng, lead, main, after):
    lead(0, 0)
    main(0, 0)
    with eng.Fori(0, (UNITS - 1) // 2) as i:
        for q in (1, 0):
            j = 2 * i + (2 - q)
            lead(j, q)
            after(2 * i + (1 - q), 1 - q)
            main(j, q)
    after(UNITS - 1, 0)


def nothing(j, q):
    pass


class Count:

    def __init__(self, eng, sem):
        self.eng, self.sem, self.n, self.over = eng, sem, 0, None

    def mark(self, ins):
        ins.then_inc(self.sem, 1)
        self.n += 1

    def value(self, back=0):
        n = self.n - back
        return n if self.over is None else self.over[0] * self.over[1] + n

    def wait(self, back=0):
        self.eng.wait_ge(self.sem, self.value(back))

    @contextmanager
    def loop(self, start, end, per):
        base = self.n
        with self.eng.Fori(start, end) as i:
            self.over, self.n = (i, per), base - start * per
            yield i
            assert self.n == base - start * per + per, (self.n, base, per)
        self.over, self.n = None, base + (end - start) * per


def carve(arena):
    at = [0]

    def take(parts, shape, dtype):
        size = 1
        for s in shape:
            size *= s
        words = -(-size * (2 if dtype in (BF16, F16, U16) else 4) // 32) * 8
        ap = arena[0:parts, at[0]:at[0] + words]
        at[0] += words
        assert at[0] <= arena.shape[1], at[0]
        if dtype != F32:
            ap = ap.bitcast(dtype)
        ap = ap[:, 0:size]
        if len(shape) > 1:
            names = "abcd"[:len(shape)]
            ap = ap.rearrange(f"p ({' '.join(names)}) -> p {' '.join(names)}",
                              **{n: s for n, s in zip(names, shape)})
        return ap
    return take, at


def build_adjacency(nc, io, sems, persist, take, psum):
    src, dst, ew, W_adj, C_adj, keys = (io[k] for k in ("src", "dst", "ew", "W_adj", "C_adj", "keys"))
    idx, cnt, deg = persist["idx"], persist["cnt"], persist["deg"]
    psS = psum[:, 0:3, :]
    psD = psum[:, 3, :]
    zero = take(P, [NP], F32)
    ends = take(EP, [2, TILES], I32)
    w = take(EP, [TILES], F32)
    cell, key, tmp, tmp2, flip, spare = (take(EP, [TILES], I32) for _ in range(6))
    spare0 = take(EP, [TB], I32)
    dlo, dhi = take(EP, [TILES], BF16), take(EP, [TILES], BF16)
    V = take(EP, [TILES, 5], BF16)
    rest = take(EP, [TILES], F32)
    ramp, rampb = take(P, [P], F32), take(P, [P], BF16)
    pcol = take(P, [1], F32)
    earlier = take(EP, [EP], BF16)
    krow = take(EP, [3, B], F32)
    Eq = take(EP, [3, TB * (B + 1)], BF16)
    Et = take(EP, [3, TB, EP], BF16)
    ohl, ohh, ohv = take(EP, [3, TB, P], BF16), take(EP, [3, TB, CHUNKS], BF16), take(EP, [3, TB, 4, CHUNKS], BF16)
    mask = take(EP, [TB], I32)
    wsum = take(EP, [TILES], F32)
    cell_slot, w_slot = take(EP, [2, TB], I32), take(EP, [2, TB], F32)
    nudge = take(EP, [8], F32)
    names = "edges_in ramps zero_set c_zeroed key_set keys_out row_used equal_set batch_counted cell_set " \
            "w_added slot_filled dve_step merged hot_set"
    s = {n: sems(n) for n in names.split()}
    row_in = [sems(f"row_in{i}") for i in range(3)]
    w_zeroed = [sems(f"w_zeroed{i}") for i in range(2)]

    block = nc.Block()
    with block:
        @block.sync
        def _(sp):
            for to, of in ((ends[:, 0, :], src), (ends[:, 1, :], dst), (w, ew)):
                sp.dma_start(to, of.rearrange("(p t) -> p t", t=TILES)).then_inc(s["edges_in"], 16)
            sp.wait_ge(s["keys_out"], 16)
            sp.wait_ge(s["zero_set"], 1)
            W_rows = W_adj[0:DUMP, :].rearrange("(r c) o -> r (c o)", c=NP)
            for u in range(2):
                sp.dma_start(W_rows[u * P:(u + 1) * P, :], zero).then_inc(w_zeroed[u], 16)
            with sp.Fori(1, CHUNKS // 2) as k:
                for u in range(2):
                    sp.wait_ge(w_zeroed[u], 16 * k)
                    sp.dma_start(W_rows[ds((2 * k + u) * P, P), :], zero).then_inc(w_zeroed[u], 16)
            sp.dma_start(W_rows[NP - P:, :], zero).then_inc(w_zeroed[0], 16)
            sp.dma_start(W_adj[DUMP:DUMP + SPARE, :].rearrange("(p c) o -> p (c o)", c=8),
                         zero[:, 0:8]).then_inc(w_zeroed[1], 16)
            for u in range(2):
                sp.wait_ge(w_zeroed[u], 16 * (CHUNKS // 2 + 1))
            C_rows = C_adj[0:DUMP, :].rearrange("(r c) o -> r (c o)", c=NP)
            z16 = zero[0:P // 2, 0:NP // 2].bitcast(F16)
            sp.dma_start(C_adj[DUMP:DUMP + SPARE, :].rearrange("(p c) o -> p (c o)", c=16),
                         z16[:, 0:16]).then_inc(s["c_zeroed"], 16)
            with sp.Fori(0, 2 * CHUNKS) as k:
                sp.wait_ge(s["c_zeroed"], 16 * k + 16)
                sp.dma_start(C_rows[ds(k * (P // 2), P // 2), :], z16).then_inc(s["c_zeroed"], 16)
            sp.wait_ge(s["c_zeroed"], 16 * (2 * CHUNKS + 1))

        @block.scalar
        def _(act):
            act.wait_ge(s["key_set"], 1)
            act.dma_start(keys.rearrange("b p j -> p b j"),
                          key.rearrange("p (b j) -> p b j", j=TB)).then_inc(s["keys_out"], 16)
            act.wait_ge(s["keys_out"], 16)
            rows = keys.rearrange("b p j -> b (p j)")

            def row(b, slot):
                act.dma_start(krow[:, slot, :].bitcast(I32),
                              rows[ds(b, 1), :].to_broadcast([EP, B])).then_inc(row_in[slot], 16)

            for b in range(3):
                row(b, b)
            with act.Fori(0, (NB - 4) // 3) as i:
                for u in range(3):
                    act.wait_ge(s["row_used"], 3 * i + u + 1)
                    row(3 * i + 3 + u, u)
            act.wait_ge(s["row_used"], NB - 3)
            row(NB - 1, (NB - 1) % 3)

        @block.gpsimd
        def _(pool):
            for to, step in ((ramp, 0), (pcol, 1)):
                pool.iota(to, [[1, to.shape[1]]], base=0, channel_multiplier=step,
                          allow_small_or_imprecise_dtypes=True).then_inc(s["ramps"], 1)
            pool.iota(spare0, [[1, TB]], base=0, channel_multiplier=TB).then_inc(s["ramps"], 1)
            pool.memset(nudge, 0.0).then_inc(s["ramps"], 1)
            pool.wait_ge(s["ramps"], 4)
            for u in range(2):
                pool.wait_ge(w_zeroed[u], 16 * (CHUNKS // 2 + 1))
            add_batches(pool, W_adj, idx, wsum, F32, cell_slot, w_slot, nudge,
                        s["cell_set"], s["slot_filled"], s["w_added"])

        @block.vector
        def _(dve):
            step = Count(dve, s["dve_step"])

            def link(ins):
                step.mark(ins)
                step.wait()

            dve.memset(zero, 0.0).then_inc(s["zero_set"], 1)
            dve.wait_ge(s["edges_in"], 48)
            link(dve.tensor_scalar(tmp, ends[:, 0, :], float(CHUNKS), None, ALU.mult))
            link(dve.tensor_scalar(tmp2, ends[:, 1, :], 7, None, ALU.logical_shift_right))
            dve.tensor_copy(dhi, tmp2)
            link(dve.tensor_tensor(tmp, tmp, tmp2, ALU.add))
            link(dve.tensor_scalar(tmp, tmp, 7, None, ALU.logical_shift_left))
            link(dve.tensor_scalar(tmp2, ends[:, 1, :], P - 1, None, ALU.bitwise_and))
            dve.tensor_copy(dlo, tmp2)
            link(dve.tensor_tensor(cell, tmp, tmp2, ALU.bitwise_or))
            dve.tensor_scalar(key, cell, KEY_BIT, None, ALU.bitwise_or).then_inc(s["key_set"], 1)
            dve.wait_ge(s["ramps"], 4)
            link(dve.tensor_scalar(spare0, spare0, DUMP, None, ALU.bitwise_or))
            link(dve.tensor_copy(spare.bitcast(U16).rearrange("p (b j) -> p b j", j=2 * TB),
                                 spare0.bitcast(U16).unsqueeze(1).to_broadcast([EP, NB, 2 * TB])))
            dve.tensor_tensor(flip, cell, spare, ALU.bitwise_xor)
            link(dve.tensor_copy(V[:, :, 0], w))
            link(dve.tensor_tensor(rest, w, V[:, :, 0], ALU.subtract))
            link(dve.tensor_copy(V[:, :, 1], rest))
            link(dve.tensor_tensor(rest, rest, V[:, :, 1], ALU.subtract))
            dve.tensor_copy(V[:, :, 2], rest)
            dve.memset(V[:, :, 3:5], 1.0)
            dve.tensor_copy(rampb, ramp)
            dve.memset(Eq.rearrange("p a b -> p (a b)"), 0.0)
            link(dve.tensor_scalar(earlier, ramp[0:EP, 0:EP], pcol[0:EP, 0:1], None, ALU.is_gt))
            keyf = key.bitcast(F32)

            def compare(b, slot, arrivals):
                dve.wait_ge(row_in[slot], 16 * arrivals)
                if not isinstance(b, int) or b >= 3:
                    dve.wait_ge(s["batch_counted"], b - 2)
                for j in range(TB):
                    ins = dve.tensor_scalar(Eq[:, slot, j * B:(j + 1) * B], krow[:, slot, :],
                                            keyf[:, ds(b * TB + j, 1)], None, ALU.is_equal)
                ins.then_inc(s["row_used"], 1)
                dve.tensor_tensor(ohl[:, slot], rampb[0:EP, :].unsqueeze(1).to_broadcast([EP, TB, P]),
                                  dlo[:, ds(b * TB, TB)].unsqueeze(2).to_broadcast([EP, TB, P]), ALU.is_equal)
                dve.tensor_tensor(ohh[:, slot], rampb[0:EP, 0:CHUNKS].unsqueeze(1).to_broadcast([EP, TB, CHUNKS]),
                                  dhi[:, ds(b * TB, TB)].unsqueeze(2).to_broadcast([EP, TB, CHUNKS]),
                                  ALU.is_equal).then_inc(s["hot_set"], 1)
                dve.wait_ge(s["row_used"], b + 1)
                own = Eq[:, slot, :].rearrange("p (j k) -> p j k", k=B + 1)[:, :, 0:B] \
                    .rearrange("p j (q i) -> p j q i", i=TB)[:, :, :, 0]
                dve.tensor_tensor(Et[:, slot], own, earlier.unsqueeze(1).to_broadcast([EP, TB, EP]), ALU.mult)
                dve.wait_ge(s["hot_set"], b + 1)
                dve.tensor_tensor(ohv[:, slot], ohh[:, slot].unsqueeze(2).to_broadcast([EP, TB, 4, CHUNKS]),
                                  V[:, ds(b * TB, TB), 0:4].unsqueeze(3).to_broadcast([EP, TB, 4, CHUNKS]),
                                  ALU.mult).then_inc(s["equal_set"], 1)

            def merge(b, slot):
                dve.wait_ge(s["batch_counted"], b + 1)
                sums = psS[0:EP, slot, 0:TB * 5].rearrange("p (i c) -> p i c", c=5)
                at = ds(b * TB, TB)
                dve.tensor_reduce(wsum[:, at], sums[:, :, 0:3], AX, ALU.add)
                dve.tensor_scalar(cnt[:, at], sums[:, :, 3], HALF, None, ALU.mult)
                if not isinstance(b, int) or b >= 1:
                    dve.wait_ge(s["cell_set"], b)
                dve.tensor_scalar(mask, sums[:, :, 4], 0.0, -1.0, ALU.is_equal, ALU.mult).then_inc(s["merged"], 1)
                dve.wait_ge(s["merged"], 2 * b + 1)
                dve.tensor_tensor(mask, mask, flip[:, at], ALU.bitwise_and).then_inc(s["merged"], 1)
                dve.wait_ge(s["merged"], 2 * b + 2)
                dve.tensor_tensor(idx[:, at], mask, spare[:, at], ALU.bitwise_xor).then_inc(s["cell_set"], 1)

            compare(0, 0, 1)
            for b in range(3):
                compare(b + 1, (b + 1) % 3, 1 + (b == 2))
                merge(b, b)
            with dve.Fori(1, NB // 3) as i:
                for u in range(3):
                    compare(3 * i + 1 + u, (1 + u) % 3, i + 1 + (u == 2))
                    merge(3 * i + u, u)
            merge(NB - 1, (NB - 1) % 3)
            parts = psD[:, 0:4 * CHUNKS].rearrange("p (c k) -> p c k", c=4)
            link(dve.tensor_copy(deg[:, 0:4, :], parts))
            link(dve.tensor_tensor(deg[:, 0, :], deg[:, 0, :], deg[:, 1, :], ALU.add))
            link(dve.tensor_tensor(deg[:, 0, :], deg[:, 0, :], deg[:, 2, :], ALU.add))

        @block.tensor
        def _(pe):
            pe.wait_ge(s["zero_set"], 1)
            pe.matmul(psD[:, 0:4 * CHUNKS], zero[:, 0:P], zero[:, 0:4 * CHUNKS], start=True, stop=False,
                      skip_group_check=True)

            def batch(b, slot):
                pe.wait_ge(s["equal_set"], b + 1)
                if not isinstance(b, int) or b >= 3:
                    pe.wait_ge(s["cell_set"], b - 2)
                for i in range(TB):
                    for j in range(TB):
                        same = Eq[:, slot, j * B:(j + 1) * B].rearrange("p (q i) -> p q i", i=TB)[:, :, i]
                        n = 5 if j < i else 4
                        pe.matmul(psS[0:EP, slot, 5 * i:5 * i + n], same,
                                  V[:, ds(b * TB + j, 1), 0:n].rearrange("p a c -> p (a c)"),
                                  start=(j == 0), stop=False, skip_group_check=True)
                    pe.matmul(psS[0:EP, slot, 5 * i + 4:5 * i + 5], Et[:, slot, i, :], V[:, 0, 4:5],
                              start=False, stop=(i == TB - 1), skip_group_check=True)
                for j in range(TB):
                    ins = pe.matmul(psD[:, 0:4 * CHUNKS], ohl[:, slot, j, :],
                                    ohv[:, slot, j].rearrange("p c k -> p (c k)"),
                                    start=False, stop=False, skip_group_check=True)
                ins.then_inc(s["batch_counted"], 1)

            for b in range(4):
                batch(b, b % 3)
            with pe.Fori(1, NB // 3) as i:
                for u in range(3):
                    batch(3 * i + 1 + u, (1 + u) % 3)


def add_batches(pool, table, idx, values, dtype, cell_slot, value_slot, nudge, cell_set, slot_filled, added):
    idx16 = idx.bitcast(U16)
    slots16 = cell_slot.rearrange("p a b -> p (a b)").bitcast(U16)

    def batch(b, slot, first=False):
        if cell_set is not None:
            pool.wait_ge(cell_set, b + 1)
        pool.tensor_copy(slots16[:, slot * 2 * TB:(slot + 1) * 2 * TB],
                         idx16[:, ds(b * 2 * TB, 2 * TB)]).then_inc(slot_filled, 1)
        pool.tensor_copy(value_slot[:, slot, :], values[:, ds(b * TB, TB)]).then_inc(slot_filled, 1)
        pool.wait_ge(slot_filled, 3 * b + 2)
        if not first:
            pool.wait_ge(added, 16 * TB * b)
        pool.tensor_tensor(nudge, nudge, nudge, ALU.add).then_inc(slot_filled, 1)
        pool.wait_ge(slot_filled, 3 * b + 3) if first else None
        for j in range(TB):
            pool.indirect_dma_start(table, bass.IndirectOffsetOnAxis(cell_slot[:, slot, j:j + 1], 0),
                                    value_slot[:, slot, j:j + 1], None, compute_op=ALU.add).then_inc(added, 16)

    batch(0, 0, True)
    batch(1, 1)
    with pool.Fori(1, NB // 2) as i:
        batch(2 * i, 0)
        batch(2 * i + 1, 1)
    pool.wait_ge(added, 16 * TB * NB)


def stage_list():
    stages = [("start", None, (True, None, True)), ("gcn", 0, (True, None, True)), ("gcn", 1, (True, None, True)),
              ("gcn", 2, (False, "ln", False)),
              ("sage", 0, None), ("split", 0, (False, 0, False)),
              ("sage", 1, None), ("encode", None, None), ("split", 1, (False, 1, False))]
    stages += [("gru", n, (False, 1, False)) for n in range(STEPS - 1)]
    return stages + [("gru", STEPS - 1, None), ("decode", None, (False, "ln", True)), ("last", None, None)]


class Bases:

    def __init__(self):
        self.products = self.read = self.seconds = 1
        self.features = self.inputs = self.gates = self.norms = 0
        self.used, self.sweep, self.selfs, self.sum_dve, self.sum_act = USED0, 0, 0, 0, 0

    def advance(self, name, arg, feeds):
        has = lambda *names: UNITS if name in names else 0
        self.products += has("gcn", "sage", "gru", "decode", "last", "encode")
        self.seconds += has("sage", "split", "decode", "encode") + (UNITS if (name, arg) in
                                                           [("gcn", 2)] + [("gru", n) for n in range(STEPS - 1)] else 0)
        self.features += UNITS if feeds else 0
        self.inputs += has("gcn", "sage", "last", "split")
        self.gates += has("gru")
        self.norms += UNITS if (name, arg) in (("gcn", 2), ("sage", 1)) or name in ("decode", "last") else 0
        self.read += has("gcn", "sage", "gru", "last")


def run_layers(nc, io, sems, persist, take, at, psum):
    W_adj, C_adj = io["W_adj"], io["C_adj"]
    idx, cnt, deg = persist["idx"], persist["cnt"], persist["deg"]
    top = at[0]
    ring32 = take(P, [LAP + 1, SLOT], F32)
    end = at[0]
    at[0] = top
    ring16 = take(P, [LAP + 1, SLOT], F16)
    h_fm = take(P, [PAD * P], F32)
    gate_r, gate_z, pre_n, new_n, diff = (take(P, [BANK], F32) for _ in range(5))
    at[0] = max(end, at[0])
    x_nm = take(P, [PAD, D], F32)
    top = at[0]
    h_nm = take(P, [PAD, D], F32)
    at[0] = top
    h_parts = take(P, [2, PAD * P], F16)
    sum_fm = take(P, [PAD * P], F32)
    top = at[0]
    chunk32 = take(P, [LAP, D], F32)
    at[0] = top
    own_in = take(P, [2, BANK], F32)
    sum_in = take(P, [2, BANK], F32)
    unit_out = take(P, [2, UC, D], F32)
    work = take(P, [UC, D], F32)
    weights = take(P, [len(WEIGHTS), D], F32)
    wt = {n: weights[:, i, :] for i, n in enumerate(WEIGHTS)}
    wih = weights[:, WEIGHTS.index("wihT0"):WEIGHTS.index("wihT0") + 3, :].rearrange("p w f -> p (w f)")
    rows = take(P, [len(ROWS), D], F32)
    row = {n: rows[:, i, :] for i, n in enumerate(ROWS)}
    cols = take(P, [len(COLS)], F32)
    col = {n: cols[:, i:i + 1] for i, n in enumerate(COLS)}
    br, bz = take(P, [1], F32), take(P, [1], F32)
    W3l, gates = take(P, [D], F32), take(P, [3 * D], F32)
    b3wide = unit_out[:, 0, 0, :]
    row3l = take(P, [D], F32)
    ident, ident16 = take(P, [P], F32), take(P, [P], F16)
    dinv_w, dinv_c, rdeg, dmask = (take(P, [PAD], F32) for _ in range(4))
    stats, meanvar = take(P, [UC, 6], F32), take(P, [UC, 2], F32)
    std, rstd = take(P, [UC], F32), take(P, [UC], F32)
    eps = take(P, [1], F32)
    extremes, peak, top_abs = take(P, [2], F32), take(P, [2], F32), take(P, [1], F32)
    expo, expo2 = take(P, [1], I32), take(P, [1], I32)
    up, down = take(P, [2], F32), take(P, [2], F32)
    cell_slot, c_slot = take(EP, [2, TB], I32), take(EP, [2, TB], F16)
    nudge = take(EP, [8], F32)
    tick = take(P, [8], F32)

    names = "loaded ident_set slot_filled c_added pad_zeroed b3_spread deg_set deg_root consts_set out_written " \
            "products products_read seconds seconds_read inputs_set features_set chunk_used chunk_set selfs_added " \
            "sum_dve sum_act hi_set var_set std_set gates_set pre_set new_set unit_set kept dve_step " \
            "dve_stage act_stage ext_set peak_set probs_in probs_set"
    s = {n: sems("l_" + n) for n in names.split()}
    landed = [sems(f"landed{i}") for i in range(LAP + 1)]
    stages = stage_list()

    def unit(ap, j):
        return ap[:, ds(j * BANK, BANK)]

    def nodes(ap, j):
        return ap[:, ds(j * UC, UC), :]

    def bank_nm(b):
        return psum[:, b, :].rearrange("p (c f) -> p c f", f=D)

    block = nc.Block()
    with block:
        @block.gpsimd
        def _(pool):
            pool.memset(ident, 1.0).then_inc(s["ident_set"], 1)
            pool.memset(nudge, 0.0).then_inc(s["kept"], 1)
            pool.wait_ge(s["ident_set"], 1)
            pool.affine_select(out=ident, in_=ident, compare_op=ALU.is_equal, fill=0.0, base=0,
                               pattern=[[-1, P]], channel_multiplier=1).then_inc(s["ident_set"], 1)
            add_batches(pool, C_adj, idx, cnt, F16, cell_slot, c_slot, nudge, None, s["slot_filled"], s["c_added"])
            scales = 0
            for k, (name, arg, feeds) in enumerate(stages):
                if (name, arg) in (("gcn", 2), ("sage", 1)) or name == "decode":
                    before = units_before(stages, k)
                    bias = {"gcn": row["sb2"], "sage": None, "decode": row["b4"]}[name]

                    def keep(j, q):
                        pool.wait_ge(s["unit_set"], j + (before + 1))
                        if bias is None:
                            ins = pool.tensor_copy(nodes(x_nm, j), unit_out[:, q])
                        else:
                            ins = pool.tensor_tensor(nodes(x_nm, j), unit_out[:, q],
                                                     bias.unsqueeze(1).to_broadcast([P, UC, D]), ALU.add)
                        ins.then_inc(s["kept"], 1)
                    walk(pool, nothing, keep, nothing)
                if name == "split":
                    scales += 1
                    pool.wait_ge(s["ext_set"], scales)
                    pool.partition_all_reduce(peak, extremes, P, bass.bass_isa.ReduceOp.absmax) \
                        .then_inc(s["peak_set"], 1)

        @block.sync
        def _(sp):
            x = io["x"]
            sp.dma_start(x_nm[:, 0:CHUNKS - 1, :],
                         x[0:(CHUNKS - 1) * P, :].rearrange("(c p) f -> p c f", p=P)).then_inc(s["loaded"], 16)
            sp.wait_ge(s["pad_zeroed"], 1)
            sp.dma_start(x_nm[0:TAIL, CHUNKS - 1, :], x[(CHUNKS - 1) * P:, :]).then_inc(s["loaded"], 16)
            sp.dma_start(weights, io["weights"].rearrange("w p f -> p w f")).then_inc(s["loaded"], 16)
            sp.dma_start(rows, io["rows"].rearrange("r f -> (r f)").unsqueeze(0).to_broadcast([P, len(ROWS) * D])
                         .rearrange("p (r f) -> p r f", f=D)).then_inc(s["loaded"], 16)
            sp.dma_start(cols, io["cols"]).then_inc(s["loaded"], 16)
            used, wide_before = USED0, True
            for _, _, feeds in stages:
                if feeds is None:
                    continue
                wide = feeds[0]
                table, ring = (W_adj, ring32) if wide else (C_adj, ring16)
                table = table[0:DUMP, :].rearrange("(r c) o -> r (c o)", c=NP)
                if wide_before and not wide:
                    sp.wait_ge(s["chunk_used"], used)
                    sp.wait_ge(s["c_added"], 16 * TB * NB)
                wide_before = wide
                for first, n, _ in SWEEPS:
                    c0 = first * BANK
                    width = min(n * BANK, NP - c0)

                    def load(c, slot):
                        sp.dma_start(ring[:, slot, 0:width], table[ds(c * P, P), c0:c0 + width]) \
                            .then_inc(landed[slot], 16)

                    if used > CHUNKS:
                        sp.wait_ge(s["chunk_used"], used - CHUNKS + 1)
                    load(0, LAP)
                    with sp.Fori(0, LAPS) as i:
                        for u in range(LAP):
                            sp.wait_ge(s["chunk_used"], i * LAP + (used + u - LAP + 2))
                            load(i * LAP + (u + 1), u)
                    used += CHUNKS
            out = io["out"]
            norms = units_before(stages, len(stages) - 1)
            with sp.Fori(0, UNITS - 1) as j:
                sp.wait_ge(s["unit_set"], j + (norms + 1))
                sp.dma_start(out[ds(j * BANK, BANK), :].rearrange("(c p) f -> p c f", p=P),
                             nodes(h_nm, j)).then_inc(s["out_written"], 16)
            sp.wait_ge(s["unit_set"], norms + UNITS)
            sp.dma_start(out[(CHUNKS - 1) * P:, :], h_nm[0:TAIL, CHUNKS - 1, :]).then_inc(s["out_written"], 16)
            sp.wait_ge(s["out_written"], 16 * UNITS)

        @block.tensor
        def _(pe):
            base = Bases()
            pe.wait_ge(s["loaded"], 80)
            pe.wait_ge(s["b3_spread"], 1)
            pe.matmul(psum[:, 4, 0:D], wt["W3T"], wt["Wl"], start=True, stop=True).then_inc(s["products"], 1)
            pe.matmul(psum[:, 6, 0:D], wt["W3T"], wt["Wl"], start=True, stop=True).then_inc(s["seconds"], 1)
            pe.matmul(psum[:, 5, 0:D], b3wide, wt["Wl"], start=True, stop=True).then_inc(s["chunk_used"], USED0)
            for k, (name, arg, feeds) in enumerate(stages):
                if k:
                    pe.wait_ge(s["dve_stage"], k)
                    pe.wait_ge(s["act_stage"], k)

                base_units, base_new = units_before(stages, k), new_before(stages, k)

                def wait_read(j, behind):
                    if isinstance(j, int) and j < behind:
                        return
                    if name in ("encode", "decode"):
                        pe.wait_ge(s["new_set"], j + (base_new + 1 - behind))
                    else:
                        pe.wait_ge(s["products_read"], j + (base.read + 1 - behind))

                def products(j, q):
                    if name in ("gcn", "last", "sage"):
                        wait_read(j, 2)
                        pe.wait_ge(s["inputs_set"], j + (base.inputs + 1))
                        for c in range(UC):
                            sl = slice(c * D, (c + 1) * D)
                            if name == "sage":
                                own, near = (("W1s", "W1n"), ("W2s", "W2n"))[arg]
                                pe.matmul(psum[:, 6 + q, sl], own_in[:, q, sl], wt[own], start=True, stop=True)
                                rhs = wt[near]
                            else:
                                rhs = wt["L3W"] if name == "last" else (wt["W1"], wt["W2"], W3l)[arg]
                            ins = pe.matmul(psum[:, 4 + q, sl], sum_in[:, q, sl], rhs, start=True, stop=True)
                        ins.then_inc(s["products"], 1)
                    elif name == "encode":
                        wait_read(j, 2)
                        pe.matmul(psum[:, 4 + q, :], wt["E1T"], unit(h_fm, j), start=True, stop=True) \
                            .then_inc(s["products"], 1)
                    elif name == "decode":
                        wait_read(j, 2)
                        pe.matmul(psum[:, 4 + q, :], wt["D1T"], unit(h_fm, j), start=True, stop=True) \
                            .then_inc(s["products"], 1)
                    elif name == "gru":
                        wait_read(j, 1)
                        if feeds and not (isinstance(j, int) and j < 2):
                            pe.wait_ge(s["seconds_read"], j + (base.seconds - 1))
                        for gate in range(2):
                            pe.matmul(psum[:, 4 + gate, :], gates[:, gate * D:(gate + 1) * D], unit(sum_fm, j),
                                      start=True, stop=False)
                            pe.matmul(psum[:, 4 + gate, :], wt[f"whhT{gate}"], unit(h_fm, j), start=False,
                                      stop=True).then_inc(s["probs_in"], 1)
                        pe.matmul(psum[:, 6, :], wt["whhT2"], unit(h_fm, j), start=True, stop=True)
                        pe.matmul(psum[:, 7, :], gates[:, 2 * D:], unit(sum_fm, j), start=True, stop=True) \
                            .then_inc(s["products"], 1)

                def seconds(j, q):
                    def wait_second(behind):
                        if isinstance(j, int) and j < behind:
                            return
                        pe.wait_ge(s["seconds_read"], j + (base.seconds + 1 - behind))

                    if (name, arg) == ("gcn", 2) or name == "sage":
                        bank = 6 + q if name == "gcn" else q
                        wait_second(2)
                        pe.wait_ge(s["unit_set"], j + (base_units + 1))
                        for c in range(UC):
                            ins = pe.transpose(psum[:, bank, c * P:(c + 1) * P], unit_out[:, q, c, :], ident)
                        ins.then_inc(s["seconds"], 1)
                    elif name == "split":
                        wait_second(2)
                        pe.wait_ge(s["inputs_set"], j + (base.inputs + 1))
                        for c in range(UC):
                            ins = pe.transpose(psum[:, 4 + q, c * P:(c + 1) * P], sum_in[:, q, c * P:(c + 1) * P], ident)
                        ins.then_inc(s["seconds"], 1)
                    elif name == "encode":
                        wait_second(2)
                        pe.wait_ge(s["new_set"], j + (base_new + 1))
                        pe.matmul(psum[:, 6 + q, :], wt["E2T"], unit(sum_fm, j), start=True, stop=True) \
                            .then_inc(s["seconds"], 1)
                    elif name == "decode":
                        wait_second(2)
                        pe.wait_ge(s["new_set"], j + (base_new + 1))
                        for c in range(UC):
                            ins = pe.matmul(psum[:, 6 + q, c * D:(c + 1) * D], own_in[:, q, c * P:(c + 1) * P],
                                            wt["D2T"], start=True, stop=True)
                        ins.then_inc(s["seconds"], 1)
                    elif name == "gru" and feeds:
                        pe.wait_ge(s["unit_set"], j + (base_units + 1))
                        if not (isinstance(j, int) and j == UNITS - 1):
                            pe.wait_ge(s["gates_set"], 2 * j + (2 * base.gates + 3))
                        else:
                            wait_second(1)
                        for c in range(UC):
                            ins = pe.transpose(psum[:, 4, c * P:(c + 1) * P],
                                               unit_out[:, q].rearrange("p c f -> p (c f)")[:, c * P:(c + 1) * P], ident)
                        ins.then_inc(s["seconds"], 1)

                def chunk(c, slot, sweep, arrivals, begin=False, unit_of=None):
                    first, n, bank = SWEEPS[sweep]
                    pe.wait_ge(landed[slot], arrivals)
                    if wide:
                        pe.wait_ge(s["chunk_set"], c + (base.used - USED0 + 1))
                    elif unit_of is not None:
                        pe.wait_ge(s["features_set"], unit_of)
                    ring = ring32 if wide else ring16
                    slot32 = LAP - 1 if slot == LAP else slot
                    for part in range(1 if wide else 2):
                        for b in range(n):
                            width = block_width(first + b)
                            lhs = chunk32[:, slot32, :] if wide else h_parts[:, part, ds(c * P, P)]
                            ins = pe.matmul(psum[:, bank + b, 0:width], lhs, ring[:, slot, b * BANK:b * BANK + width],
                                            start=begin and part == 0, stop=False, skip_group_check=True)
                    ins.then_inc(s["chunk_used"], 1)

                def own_features(sweep):
                    first, n, bank = SWEEPS[sweep]
                    for c in range(first * UC, min((first + n) * UC, CHUNKS)):
                        to = psum[:, bank + c // UC - first, c % UC * P:c % UC * P + P]
                        for part in range(1 if wide else 2):
                            lhs = h_nm[:, c, :] if wide else h_parts[:, part, c * P:(c + 1) * P]
                            ins = pe.matmul(to, lhs, ident if wide else ident16, start=False, stop=False,
                                            skip_group_check=True)
                    ins.then_inc(s["selfs_added"], 1)

                if not feeds:
                    products(0, 0)
                    with pe.Fori(0, (UNITS - 1) // 2) as i:
                        for q in (1, 0):
                            products(2 * i + (2 - q), q)
                            seconds(2 * i + (1 - q), 1 - q)
                    seconds(UNITS - 1, 0)
                    base.advance(name, arg, feeds)
                    continue

                wide, scale, selfs = feeds
                laps = LAPS * base.sweep
                feat = base.features

                def run(i, half, c0):
                    for u in range(4):
                        c = c0 + u
                        need = (i * 2 + (half + (u == 3))) + (feat + 1)
                        chunk(c, 4 * half + u, 0, 16 * i + 16 * (laps + 1), False, need)

                products(0, 0)
                products(1, 1)
                seconds(0, 0)
                chunk(0, LAP, 0, 16 * (base.sweep + 1), True, feat + 1)
                with pe.Fori(0, (UNITS - 3) // 2) as i:
                    for q in (0, 1):
                        products(2 * i + (2 + q), q)
                        seconds(2 * i + (1 + q), 1 - q)
                        run(i, q, i * LAP + (4 * q + 1))
                products(UNITS - 1, 0)
                seconds(UNITS - 2, 1)
                run(LAPS - 1, 0, LAP * (LAPS - 1) + 1)
                seconds(UNITS - 1, 0)
                run(LAPS - 1, 1, LAP * (LAPS - 1) + 5)
                for sweep in range(len(SWEEPS)):
                    if sweep:
                        if sweep == 1:
                            pe.wait_ge(s["features_set"], feat + UNITS)
                            if (name, arg) == ("gcn", 2):
                                pe.wait_ge(s["seconds_read"], base.seconds + UNITS)
                        else:
                            pe.wait_ge(s["sum_dve"], base.sum_dve_before) if base.sum_dve_before else None
                            pe.wait_ge(s["sum_act"], base.sum_act_before) if base.sum_act_before else None
                        laps = LAPS * base.sweep
                        chunk(0, LAP, sweep, 16 * (base.sweep + 1), True)
                        with pe.Fori(0, LAPS) as i:
                            for u in range(LAP):
                                chunk(i * LAP + (u + 1), u, sweep, 16 * i + 16 * (laps + 1))
                    elif (name, arg) in NEXT_GRU:
                        pe.wait_ge(s["features_set"], feat + UNITS)
                        pe.matmul(psum[:, 7, 0:3 * D], wt[f"cT{NEXT_GRU[name, arg]}"], wih, start=True,
                                  stop=True).then_inc(s["probs_set"], 1)
                    if selfs:
                        own_features(sweep)
                    base.sum_dve_before, base.sum_act_before = base.sum_dve, base.sum_act
                    n = SWEEPS[sweep][1]
                    base.sum_dve += n if wide else n // 2
                    base.sum_act += 0 if wide else (n + 1) // 2
                    base.used += CHUNKS
                    base.sweep += 1
                base.advance(name, arg, feeds)

        @block.scalar
        def _(act):
            base = Bases()
            act.wait_ge(s["loaded"], 80)
            act.activation(tick[:, 5:6], cols[:, 0:1], ACT.Copy).then_inc(s["seconds_read"], 1)
            act.activation(tick[:, 6:7], cols[:, 0:1], ACT.Copy).then_inc(s["new_set"], 1)
            act.activation(b3wide, col["b3"].to_broadcast([P, D]), ACT.Copy).then_inc(s["b3_spread"], 1)
            act.wait_ge(s["deg_set"], 2)
            act.activation(dinv_w, dinv_w, ACT.Sqrt).then_inc(s["deg_root"], 1)
            act.activation(dinv_c, dinv_c, ACT.Sqrt).then_inc(s["deg_root"], 1)
            for k, (name, arg, feeds) in enumerate(stages):
                if k:
                    act.wait_ge(s["dve_stage"], k)
                    act.wait_ge(s["act_stage"], k)
                wide = feeds is not None and feeds[0]
                norm = (name, arg) in (("gcn", 2), ("sage", 1)) or name in ("decode", "last")
                base_units = units_before(stages, k)
                if name == "split":
                    act.wait_ge(s["consts_set"], arg + 1)

                def lead(j, q):
                    if name in ("gcn", "sage", "last"):
                        if not isinstance(j, int):
                            act.wait_ge(s["products"], j + (base.products - 1))
                        if name == "sage":
                            act.activation(own_in[:, q], unit(h_fm, j), ACT.Copy)
                        act.activation(sum_in[:, q], unit(sum_fm, j), ACT.Copy).then_inc(s["inputs_set"], 1)
                    elif name == "split":
                        if not isinstance(j, int):
                            act.wait_ge(s["seconds"], j + (base.seconds - 1))
                        act.activation(sum_in[:, q], unit(h_fm, j), ACT.Copy).then_inc(s["inputs_set"], 1)

                    elif name == "gru":
                        act.wait_ge(s["probs_in"], 2 * j + (2 * base.gates + 1))
                        act.activation(gate_r, psum[:, 4, :], ACT.Sigmoid, bias=br).then_inc(s["gates_set"], 1)
                        act.wait_ge(s["probs_in"], 2 * j + (2 * base.gates + 2))
                        act.activation(gate_z, psum[:, 5, :], ACT.Sigmoid, bias=bz).then_inc(s["gates_set"], 1)

                def main(j, q):
                    if name == "encode":
                        act.wait_ge(s["products"], j + (base.products + 1))
                        act.activation(unit(sum_fm, j), psum[:, 4 + q, :], ACT.Relu, bias=col["eb1"]) \
                            .then_inc(s["new_set"], 1)
                    elif name == "decode":
                        act.wait_ge(s["products"], j + (base.products + 1))
                        if not isinstance(j, int):
                            act.wait_ge(s["seconds"], j + (base.seconds - 1))
                        act.activation(own_in[:, q], psum[:, 4 + q, :], ACT.Relu, bias=col["db1"]) \
                            .then_inc(s["new_set"], 1)
                    elif name == "gru":
                        act.wait_ge(s["products_read"], j + (base.read + 1))
                        act.activation(new_n, pre_n, ACT.Tanh, bias=col["bi2"]).then_inc(s["new_set"], 1)
                        act.wait_ge(s["unit_set"], j + (base_units + 1))
                        act.activation(unit(h_fm, j), unit_out[:, q].rearrange("p c f -> p (c f)"), ACT.Copy) \
                            .then_inc(s["kept"], 1)
                    if norm and name != "decode":
                        root(j)

                def root(j):
                    act.wait_ge(s["var_set"], j + (base.norms + 1))
                    act.activation(std, meanvar[:, :, 1], ACT.Sqrt, bias=eps).then_inc(s["std_set"], 1)

                def after(j, q):
                    if (name, arg) == ("gcn", 2) or name == "sage":
                        act.wait_ge(s["seconds"], j + (base.seconds + 1))
                        act.wait_ge(s["seconds_read"], j + base.seconds)
                        act.activation(tick[:, 7:8], cols[:, 0:1], ACT.Copy)
                        act.activation(unit(h_fm, j), psum[:, 6 + q if name == "gcn" else q, :], ACT.Copy) \
                            .then_inc(s["seconds_read"], 1)
                    elif name == "split" or (name == "gru" and feeds):
                        act.wait_ge(s["seconds"], j + (base.seconds + 1))
                        bank = 4 + q if name == "split" else 4
                        which = arg if name == "split" else 1
                        act.activation(unit(h_parts[:, 0, :], j), psum[:, bank, :], ACT.Copy,
                                       scale=up[:, which:which + 1]).then_inc(s["hi_set"], 1)
                    elif name == "encode":
                        act.wait_ge(s["seconds"], j + (base.seconds + 1))
                        act.activation(unit(h_fm, j), psum[:, 6 + q, :], ACT.Identity, bias=col["eb2"]) \
                            .then_inc(s["seconds_read"], 1)
                    elif name == "decode":
                        act.wait_ge(s["seconds_read"], j + (base.seconds + 1))
                        act.activation(work, work, ACT.Sigmoid).then_inc(s["hi_set"], 1)
                        root(j)
                    if wide and name in ("start", "gcn"):
                        act.wait_ge(s["features_set"], j + (base.features + 1))
                        last = isinstance(j, int)
                        for c in ((0,) if last else range(UC)):
                            slot = (LAP - 1, 0, 1, 2)[c] if q == 0 else (3, 4, 5, 6)[c]
                            act.wait_ge(s["chunk_used"], j * UC + (base.used + c - LAP + 1))
                            at_ = ds(j * UC + c, 1)
                            act.activation(chunk32[:, slot, :], h_nm[:, at_, :].rearrange("p a f -> p (a f)"),
                                           ACT.Copy).then_inc(s["chunk_set"], 1)

                walk(act, lead, main, after)
                if feeds:
                    for sweep, (first, n, bank) in enumerate(SWEEPS):
                        if wide and sweep:
                            act.wait_ge(s["chunk_used"], base.used)
                            act.activation(chunk32[:, LAP - 1, :], h_nm[:, 0, :], ACT.Copy).then_inc(s["chunk_set"], 1)
                            with act.Fori(0, LAPS) as i:
                                for u in range(LAP):
                                    act.wait_ge(s["chunk_used"], i * LAP + (base.used + u - LAP + 2))
                                    act.activation(chunk32[:, u, :],
                                                   h_nm[:, ds(i * LAP + (u + 1), 1), :].rearrange("p a f -> p (a f)"),
                                                   ACT.Copy).then_inc(s["chunk_set"], 1)
                        base.used += CHUNKS
                        base.selfs += feeds[2]
                        if not wide:
                            act.wait_ge(s["chunk_used"], base.used)
                            if feeds[2]:
                                act.wait_ge(s["selfs_added"], base.selfs)
                            scale = 1 / (HALF * LN_SCALE) if feeds[1] == "ln" else down[:, feeds[1]:feeds[1] + 1]
                            for b in range(0, n, 2):
                                c0, width = (first + b) * BANK, block_width(first + b)
                                act.activation(sum_fm[:, c0:c0 + width], psum[:, bank + b, 0:width], ACT.Copy,
                                               scale=scale).then_inc(s["sum_act"], 1)
                base.advance(name, arg, feeds)
                act.activation(tick[:, 0:1], tick[:, 0:1], ACT.Copy).then_inc(s["act_stage"], 1)

        @block.vector
        def _(dve):
            step = Count(dve, s["dve_step"])
            base = Bases()
            scales = 0

            def link(ins):
                step.mark(ins)
                step.wait()

            def spread(ap):
                return ap.unsqueeze(2).to_broadcast([P, UC, D])

            def along(r):
                return r.unsqueeze(1).to_broadcast([P, UC, D])

            dve.memset(tick[:, 0:5], 0.0)
            dve.memset(sum_fm[:, NP:], 0.0)
            dve.memset(work.rearrange("p a b -> p (a b)"), 0.0)
            link(dve.memset(eps, EPS))
            dve.memset(x_nm[:, CHUNKS - 1:, :].rearrange("p a b -> p (a b)"), 0.0).then_inc(s["pad_zeroed"], 1)
            for t in (rdeg, dinv_w, dinv_c):
                dve.memset(t[:, CHUNKS:], 0.0)
            now = slice(0, CHUNKS)
            link(dve.tensor_scalar(rdeg[:, now], deg[:, 3, :], 1.0, None, ALU.max))
            link(dve.reciprocal(rdeg[:, now], rdeg[:, now]))
            dve.tensor_scalar(deg[:, 3, :], deg[:, 3, :], 1.0, None, ALU.add)
            link(dve.tensor_scalar(deg[:, 0, :], deg[:, 0, :], 1.0, None, ALU.add))
            dve.wait_ge(s["loaded"], 80)
            dve.tensor_tensor(br, col["bi0"], col["bh0"], ALU.add)
            dve.tensor_tensor(bz, col["bi1"], col["bh1"], ALU.add)
            link(dve.tensor_scalar(dmask[:, now], deg[:, 0, :], 0.0, None, ALU.is_gt))
            dve.wait_ge(s["ident_set"], 2)
            link(dve.tensor_scalar(ident16, ident, HALF, None, ALU.mult))
            dve.tensor_scalar(dinv_w[:, now], deg[:, 0, :], 1e-34, None, ALU.max).then_inc(s["deg_set"], 1)
            dve.tensor_scalar(dinv_c[:, now], deg[:, 3, :], 1e-34, None, ALU.max).then_inc(s["deg_set"], 1)
            dve.wait_ge(s["deg_root"], 2)
            link(dve.reciprocal(dinv_c[:, now], dinv_c[:, now]))
            link(dve.reciprocal(dinv_w[:, now], dinv_w[:, now]))
            link(dve.tensor_tensor(dinv_w[:, now], dinv_w[:, now], dmask[:, now], ALU.mult))
            dve.wait_ge(s["chunk_used"], USED0)
            dve.tensor_copy(W3l, psum[:, 4, 0:D]).then_inc(s["products_read"], 1)
            link(dve.tensor_tensor(row3l, psum[:, 5, 0:D], row["bl"], ALU.add))

            for k, (name, arg, feeds) in enumerate(stages):
                if k:
                    dve.wait_ge(s["act_stage"], k)
                    dve.wait_ge(s["dve_stage"], k)
                wide = feeds is not None and feeds[0]
                base_units, base_new = units_before(stages, k), new_before(stages, k)
                kept = 1 + UNITS * sum(((n, a) in (("gcn", 2), ("sage", 1)) or n in ("decode", "gru"))
                                   for n, a, _ in stages[:k])

                dve.wait_ge(s["kept"], kept)

                def normalise(to):
                    for c in range(UC):
                        ins = dve.bn_stats(stats[:, c, :], work[:, c, :])
                    link(ins)
                    dve.tensor_copy(tick[:, 2:3], tick[:, 1:2])
                    for c in range(UC - 1):
                        dve.bn_aggr(meanvar[:, c, :], stats[:, c, :])
                    dve.bn_aggr(meanvar[:, UC - 1, :], stats[:, UC - 1, :]).then_inc(s["var_set"], 1)
                    dve.wait_ge(s["std_set"], norm_at[0])
                    link(dve.reciprocal(rstd, std))
                    for c in range(UC):
                        ins = dve.tensor_scalar(to(c), work[:, c, :], meanvar[:, c, 0:1], rstd[:, c:c + 1],
                                                ALU.subtract, ALU.mult)
                    ins.then_inc(s["unit_set"], 1)

                norm_at = [None]

                def two_parts(of, j):
                    hi, lo = (h_parts[:, p_, :].rearrange("p (c f) -> p c f", f=D)[:, ds(j * UC, UC), :]
                              for p_ in range(2))
                    link(dve.tensor_scalar(hi, of, LN_SCALE, None, ALU.mult))
                    dve.scalar_tensor_tensor(out=lo, in0=of, scalar=LN_SCALE, in1=hi, op0=ALU.mult,
                                             op1=ALU.subtract).then_inc(s["features_set"], 1)
                    dve.wait_ge(s["features_set"], j + (base.features + 1))

                def out_free(j, seconds_of=True, kept_of=True):
                    if isinstance(j, int) and j < 2:
                        return
                    if seconds_of:
                        dve.wait_ge(s["seconds"], j + (base.seconds - 1))
                    if kept_of:
                        dve.wait_ge(s["kept"], j + (kept - 1))

                def main(j, q):
                    at_ = lambda c: ds(j * UC + c, 1)
                    norm_at[0] = j + (base.norms + 1)
                    if name == "start":
                        dve.tensor_tensor(nodes(h_nm, j), nodes(x_nm, j), spread(dinv_w[:, ds(j * UC, UC)]),
                                          ALU.mult).then_inc(s["features_set"], 1)
                    elif name == "gcn" and arg < 2:
                        dve.wait_ge(s["products"], j + (base.products + 1))
                        ps = bank_nm(4 + q)
                        for c in range(UC):
                            ins = dve.scalar_tensor_tensor(out=work[:, c, :], in0=ps[:, c, :],
                                                           scalar=dinv_w[:, at_(c)], in1=row[("b1", "b2")[arg]],
                                                           op0=ALU.mult, op1=ALU.add)
                        ins.then_inc(s["products_read"], 1)
                        dve.wait_ge(s["products_read"], j + (base.read + 1))
                        dve.scalar_tensor_tensor(out=nodes(h_nm, j), in0=work, scalar=0.0,
                                                 in1=spread(dinv_w[:, ds(j * UC, UC)]), op0=ALU.max,
                                                 op1=ALU.mult).then_inc(s["features_set"], 1)
                        dve.wait_ge(s["features_set"], j + (base.features + 1))
                    elif name in ("gcn", "last"):
                        dinv = dinv_w if name == "gcn" else dinv_c
                        dve.wait_ge(s["products"], j + (base.products + 1))
                        ps = bank_nm(4 + q)
                        for c in range(UC):
                            ins = dve.scalar_tensor_tensor(out=work[:, c, :], in0=ps[:, c, :], scalar=dinv[:, at_(c)],
                                                           in1=x_nm[:, at_(c), :].rearrange("p a f -> p (a f)"),
                                                           op0=ALU.mult, op1=ALU.add)
                        ins.then_inc(s["products_read"], 1)
                        dve.wait_ge(s["products_read"], j + (base.read + 1))
                        if name == "last":
                            normalise(lambda c: h_nm[:, at_(c), :].rearrange("p a f -> p (a f)"))
                            dve.wait_ge(s["unit_set"], j + (base_units + 1))
                        else:
                            out_free(j)
                            normalise(lambda c: unit_out[:, q, c, :])
                            dve.wait_ge(s["unit_set"], j + (base_units + 1))
                            two_parts(unit_out[:, q], j)
                    elif name == "sage":
                        dve.wait_ge(s["products"], j + (base.products + 1))
                        own, near = bank_nm(6 + q), bank_nm(4 + q)
                        for c in range(UC):
                            ins = dve.scalar_tensor_tensor(
                                out=work[:, c, :], in0=near[:, c, :], scalar=rdeg[:, at_(c)],
                                in1=row["sb1"] if arg == 0 else x_nm[:, at_(c), :].rearrange("p a f -> p (a f)"),
                                op0=ALU.mult, op1=ALU.add)
                        link(ins)
                        dve.tensor_tensor(work, work, own, ALU.add).then_inc(s["products_read"], 1)
                        dve.wait_ge(s["products_read"], j + (base.read + 1))
                        if arg == 0:
                            out_free(j, kept_of=False)
                            dve.tensor_scalar(unit_out[:, q], work, 0.0, None, ALU.max).then_inc(s["unit_set"], 1)
                        else:
                            out_free(j)
                            normalise(lambda c: unit_out[:, q, c, :])
                        dve.wait_ge(s["unit_set"], j + (base_units + 1))
                    elif name == "gru":
                        dve.wait_ge(s["products"], j + (base.products + 1))
                        dve.wait_ge(s["gates_set"], 2 * j + (2 * base.gates + 1))
                        link(dve.scalar_tensor_tensor(out=pre_n, in0=psum[:, 6, :], scalar=col["bh2"], in1=gate_r,
                                                      op0=ALU.add, op1=ALU.mult))
                        dve.wait_ge(s["gates_set"], 2 * j + (2 * base.gates + 2))
                        dve.tensor_tensor(pre_n, pre_n, psum[:, 7, :], ALU.add).then_inc(s["products_read"], 1)
                        dve.wait_ge(s["new_set"], j + (base_new + 1))
                        link(dve.tensor_tensor(diff, unit(h_fm, j), new_n, ALU.subtract))
                        link(dve.tensor_tensor(diff, diff, gate_z, ALU.mult))
                        out_free(j, seconds_of=feeds is not None)
                        to = unit_out[:, q].rearrange("p c f -> p (c f)")
                        if feeds:
                            dve.tensor_tensor(to, diff, new_n, ALU.add).then_inc(s["unit_set"], 1)
                        else:
                            link(dve.tensor_tensor(diff, diff, new_n, ALU.add))
                            dve.tensor_scalar(to, diff, 0.0, None, ALU.max).then_inc(s["unit_set"], 1)
                        dve.wait_ge(s["unit_set"], j + (base_units + 1))

                def after(j, q):
                    if name == "split" or (name == "gru" and feeds):
                        dve.wait_ge(s["hi_set"], j + (hi_before(stages, k) + 1))
                        bank = 4 + q if name == "split" else 4
                        which = arg if name == "split" else 1
                        dve.scalar_tensor_tensor(out=unit(h_parts[:, 1, :], j), in0=psum[:, bank, :],
                                                 scalar=up[:, which:which + 1], in1=unit(h_parts[:, 0, :], j),
                                                 op0=ALU.mult, op1=ALU.subtract).then_inc(s["seconds_read"], 1)
                        dve.wait_ge(s["seconds_read"], j + (base.seconds + 1))
                        dve.tensor_copy(tick[:, 3:4], tick[:, 1:2]).then_inc(s["features_set"], 1)
                    elif name == "decode":
                        norm_at[0] = j + (base.norms + 1)
                        dve.wait_ge(s["seconds"], j + (base.seconds + 1))
                        dve.tensor_tensor(work, bank_nm(6 + q), along(row["db2"]), ALU.add) \
                            .then_inc(s["seconds_read"], 1)
                        dve.wait_ge(s["hi_set"], j + (hi_before(stages, k) + 1))
                        link(dve.tensor_tensor(work, work, nodes(x_nm, j), ALU.add))
                        out_free(j, seconds_of=False)
                        normalise(lambda c: unit_out[:, q, c, :])
                        dve.wait_ge(s["unit_set"], j + (base_units + 1))
                        link(dve.tensor_tensor(work, unit_out[:, q], spread(dinv_c[:, ds(j * UC, UC)]), ALU.mult))
                        two_parts(work, j)

                if name == "split":
                    scales += 1
                    link(dve.tensor_reduce(extremes[:, 0:1], h_fm[:, 0:NP], AX, ALU.max))
                    dve.tensor_reduce(extremes[:, 1:2], h_fm[:, 0:NP], AX, ALU.min).then_inc(s["ext_set"], 1)
                    dve.wait_ge(s["peak_set"], scales)
                    link(dve.tensor_reduce(top_abs, peak, AX, ALU.max))
                    if arg == 1:
                        link(dve.tensor_scalar(top_abs, top_abs, 1.0, None, ALU.max))
                    link(dve.tensor_scalar(expo, top_abs.bitcast(I32), 23, None, ALU.logical_shift_right))
                    link(dve.tensor_scalar(expo, expo, -1.0, 268.0, ALU.mult, ALU.add))
                    link(dve.tensor_scalar(expo, expo, 240.0, None, ALU.min))
                    link(dve.tensor_scalar(expo2, expo, -1.0, 255.0, ALU.mult, ALU.add))
                    dve.tensor_scalar(up[:, arg:arg + 1].bitcast(I32), expo, 23, None, ALU.logical_shift_left)
                    link(dve.tensor_scalar(down[:, arg:arg + 1].bitcast(I32), expo2, 23, None,
                                           ALU.logical_shift_left))
                    dve.tensor_copy(tick[:, 4:5], tick[:, 1:2]).then_inc(s["consts_set"], 1)

                per = marks_per_unit(name, arg, feeds)
                start_n = step.n
                main(0, 0)
                first_marks = step.n - start_n
                with step.loop(0, (UNITS - 1) // 2, 2 * per) as i:
                    for q in (1, 0):
                        after(2 * i + (1 - q), 1 - q)
                        main(2 * i + (2 - q), q)
                after(UNITS - 1, 0)

                if name == "gcn" and arg == 1:
                    for j in range(UNITS):
                        ins = dve.tensor_tensor(nodes(x_nm, j), nodes(x_nm, j), along(row3l), ALU.add)
                    link(ins)
                if feeds:
                    for sweep, (first, n, bank) in enumerate(SWEEPS):
                        if sweep == 0 and (name, arg) in NEXT_GRU:
                            dve.wait_ge(s["probs_set"], NEXT_GRU[name, arg] + 1)
                            dve.tensor_copy(gates, psum[:, 7, 0:3 * D])
                        base.used += CHUNKS
                        base.selfs += feeds[2]
                        dve.wait_ge(s["chunk_used"], base.used)
                        if feeds[2]:
                            dve.wait_ge(s["selfs_added"], base.selfs)
                        scale = 1 / (HALF * LN_SCALE) if feeds[1] == "ln" else \
                            None if feeds[1] is None else down[:, feeds[1]:feeds[1] + 1]
                        for b in range(0, n) if wide else range(1, n, 2):
                            c0, width = (first + b) * BANK, block_width(first + b)
                            if wide:
                                ins = dve.tensor_copy(sum_fm[:, c0:c0 + width], psum[:, bank + b, 0:width])
                            else:
                                ins = dve.tensor_scalar(sum_fm[:, c0:c0 + width], psum[:, bank + b, 0:width], scale,
                                                        None, ALU.mult)
                            ins.then_inc(s["sum_dve"], 1)
                base.advance(name, arg, feeds)
                dve.tensor_copy(tick[:, 1:2], tick[:, 1:2]).then_inc(s["dve_stage"], 1)


NEXT_GRU = {("split", 1): 0} | {("gru", n): n + 1 for n in range(STEPS - 1)}


def units_before(stages, k):
    return UNITS * sum((n, a) == ("gcn", 2) or n in ("sage", "gru", "decode") for n, a, _ in stages[:k])


def new_before(stages, k):
    return 1 + UNITS * sum(n in ("encode", "gru", "decode") for n, _, _ in stages[:k])


def hi_before(stages, k):
    return UNITS * sum(n in ("split", "decode") or (n == "gru" and f is not None) for n, _, f in stages[:k])


def marks_per_unit(name, arg, feeds):
    if name == "gcn":
        return 3 if arg == 2 else 0
    return {"start": 0, "sage": 3 if arg == 1 else 1, "last": 2, "split": 0, "encode": 0,
            "gru": 3 if feeds else 4, "decode": 5}[name]


def gnn_kernel(nc, io):
    with ExitStack() as ctx:
        arena = ctx.enter_context(nc.sbuf_tensor("arena", [P, ARENA], F32))
        psum = ctx.enter_context(nc.psum_tensor("psum", [P, 8, BANK], F32))

        def sems(name):
            return ctx.enter_context(nc.semaphore(name))

        take, at = carve(arena)
        persist = dict(idx=take(EP, [TILES], I32), cnt=take(EP, [TILES], F16), deg=take(P, [4, CHUNKS], F32))
        top = at[0]
        build_adjacency(nc, io, sems, persist, take, psum)
        at[0] = top
        run_layers(nc, io, sems, persist, take, at, psum)


def kernel(**inputs):
    import numpy as np
    import concourse.bacc as bacc
    from concourse.bass_utils import run_bass_kernel_spmd

    a = {k: np.ascontiguousarray(v) for k, v in inputs.items()}
    wih, whh = a["L2_gnn_gru_wih"].reshape(3, D, D), a["L2_gnn_gru_whh"].reshape(3, D, D)
    named = {"W1": a["L0_gnn_W1"], "W2": a["L0_gnn_W2"], "W3T": a["L0_gnn_W3"].T, "Wl": a["L0_gnn_Wl"],
             "W1s": a["L1_gnn_W1_self"], "W1n": a["L1_gnn_W1_neigh"], "W2s": a["L1_gnn_W2_self"],
             "W2n": a["L1_gnn_W2_neigh"], "E1T": a["L2_gnn_enc_w1"].T, "E2T": a["L2_gnn_enc_w2"].T,
             "D1T": a["L2_gnn_dec_w1"].T, "D2T": a["L2_gnn_dec_w2"].T, "L3W": a["L3_gnn_W"]}
    for i in range(3):
        named[f"wihT{i}"], named[f"whhT{i}"] = wih[i].T, whh[i].T
    for i in range(STEPS):
        named[f"cT{i}"] = a["L2_gnn_conv_w"][i].T
    bih, bhh = a["L2_gnn_gru_bih"].reshape(3, D), a["L2_gnn_gru_bhh"].reshape(3, D)
    arrays = {
        "x": a["x"], "src": a["src"], "dst": a["dst"], "ew": a["edge_weight"],
        "weights": np.stack([named[n] for n in WEIGHTS]),
        "rows": np.stack([a["L0_gnn_b1"], a["L0_gnn_b2"], a["L0_gnn_bl"], a["L1_gnn_b1"], a["L1_gnn_b2"],
                          a["L2_gnn_dec_b2"], a["L3_gnn_b"]]),
        "cols": np.ascontiguousarray(np.stack([a["L0_gnn_b3"], a["L2_gnn_enc_b1"], a["L2_gnn_enc_b2"], *bih, *bhh,
                                               a["L2_gnn_dec_b1"]]).T),
    }
    nc = bacc.Bacc("TRN2", target_bir_lowering=False, num_devices=1)
    io = {n: nc.dram_tensor(f"in_{n}", v.shape, mybir.dt.from_np(v.dtype), kind="ExternalInput").ap()
          for n, v in arrays.items()}
    io["out"] = nc.dram_tensor("out", (N, D), F32, kind="ExternalOutput").ap()
    io["W_adj"] = nc.dram_tensor("W_adj", (DUMP + SPARE, 1), F32, kind="Internal").ap()
    io["C_adj"] = nc.dram_tensor("C_adj", (DUMP + SPARE, 1), F16, kind="Internal").ap()
    io["keys"] = nc.dram_tensor("keys", (NB, EP, TB), I32, kind="Internal").ap()
    gnn_kernel(nc, io)
    r = run_bass_kernel_spmd(nc, [{f"in_{n}": v for n, v in arrays.items()}], core_ids=[0])
    return r.results[0]["out"]
```
